# Optimizing a Trainium2 kernel written in Bass

```python
import numpy as np
import jax
import jax.numpy as jnp

def _softmax(x, axis=-1):
    return jax.nn.softmax(x, axis=axis)

def _gelu(x):
    return jax.nn.gelu(x, approximate=True)

def _silu(x):
    return jax.nn.silu(x)

def _sigmoid(x):
    return jax.nn.sigmoid(x)

def _layernorm(x, axis=-1, eps=1e-05):
    m = jnp.mean(x, axis=axis, keepdims=True)
    v = jnp.var(x, axis=axis, keepdims=True)
    return (x - m) / jnp.sqrt(v + eps)

def _scatter_add(tgt, idx, src, axis=0):
    return tgt.at[idx].add(src)

def _segment_sum(src, seg, n):
    return jax.ops.segment_sum(src, seg, n)
kernel_name = 'mk_conv_attn_hybrid_d2_conv_nchw512_r4_4c7895'

def setup_inputs(seed: int=0):
    np.random.seed(seed)
    _w = jnp.asarray

    def _rec_inputs():
        import jax
        import jax.numpy as jnp
        _gk = jax.random.key(seed)
        x = 7.22e-05 + 1 * jax.random.normal(jax.random.fold_in(_gk, 1), (4, 128, 16, 16), jnp.float32)
        return x
    x = _rec_inputs()

    def _L0_conv_setup():
        import jax, jax.numpy as jnp
        import numpy as np
        B, C, H, W = (4, 128, 16, 16)
        C8 = C // 8
        key = jax.random.key(seed)
        ks = jax.random.split(key, 8)
        s = 0.02
        return {'x': jax.random.normal(ks[0], (B, C, H, W), dtype=jnp.float32), 'wq': jax.random.normal(ks[1], (C8, C), dtype=jnp.float32) * s, 'bq': jax.random.normal(ks[2], (C8,), dtype=jnp.float32) * s, 'wk': jax.random.normal(ks[3], (C8, C), dtype=jnp.float32) * s, 'bk': jax.random.normal(ks[4], (C8,), dtype=jnp.float32) * s, 'wv': jax.random.normal(ks[5], (C, C), dtype=jnp.float32) * s, 'bv': jax.random.normal(ks[6], (C,), dtype=jnp.float32) * s, 'gamma': jax.random.normal(ks[7], (1,), dtype=jnp.float32)}
    _L0_conv_all = _L0_conv_setup()
    _L0_conv_in = {k: v for k, v in _L0_conv_all.items() if k in ('wq', 'bq', 'wk', 'bk', 'wv', 'bv', 'gamma')}
    del _L0_conv_all

    def _L1_attn_setup():
        import jax, jax.numpy as jnp
        import numpy as np
        NHEAD = 8
        key = jax.random.key(seed)
        k1, k2, k3, k4 = jax.random.split(key, 4)
        B, N, I, KQ, V = (2, 1024, 128, 128, 128)
        x = jax.random.normal(k1, (B, N, I), dtype=jnp.float32)
        Wk = jax.random.normal(k2, (I, KQ), dtype=jnp.float32) * (1.0 / np.sqrt(I))
        Wq = jax.random.normal(k3, (I, KQ), dtype=jnp.float32) * (1.0 / np.sqrt(I))
        Wv = jax.random.normal(k4, (I, V), dtype=jnp.float32) * (1.0 / np.sqrt(I))
        return {'x': x, 'Wk': Wk, 'Wq': Wq, 'Wv': Wv}
    _L1_attn_all = _L1_attn_setup()
    _L1_attn_in = {k: v for k, v in _L1_attn_all.items() if k in ('Wk', 'Wq', 'Wv')}
    del _L1_attn_all

    def _L1_ffn_setup():
        import jax, jax.numpy as jnp
        import numpy as np
        B, S, D = (8, 512, 128)
        E, K, H = (8, 2, 512)
        key = jax.random.key(seed)
        ks = jax.random.split(key, 6)
        scale = 0.02
        return {'x': jax.random.normal(ks[0], (B, S, D), dtype=jnp.float32), 'gate_w': jax.random.normal(ks[1], (E, D), dtype=jnp.float32) * scale, 'w1': jax.random.normal(ks[2], (E, H, D), dtype=jnp.float32) * scale, 'b1': jax.random.normal(ks[3], (E, H), dtype=jnp.float32) * scale, 'w2': jax.random.normal(ks[4], (E, D, H), dtype=jnp.float32) * scale, 'b2': jax.random.normal(ks[5], (E, D), dtype=jnp.float32) * scale}
    _L1_ffn_all = _L1_ffn_setup()
    _L1_ffn_in = {k: v for k, v in _L1_ffn_all.items() if k in ('gate_w', 'w1', 'b1', 'w2', 'b2')}
    del _L1_ffn_all
    return {'x': x, 'L0_conv_wq': _L0_conv_in['wq'], 'L0_conv_bq': _L0_conv_in['bq'], 'L0_conv_wk': _L0_conv_in['wk'], 'L0_conv_bk': _L0_conv_in['bk'], 'L0_conv_wv': _L0_conv_in['wv'], 'L0_conv_bv': _L0_conv_in['bv'], 'L0_conv_gamma': _L0_conv_in['gamma'], 'L1_attn_Wk': _L1_attn_in['Wk'], 'L1_attn_Wq': _L1_attn_in['Wq'], 'L1_attn_Wv': _L1_attn_in['Wv'], 'L1_ffn_gate_w': _L1_ffn_in['gate_w'], 'L1_ffn_w1': _L1_ffn_in['w1'], 'L1_ffn_b1': _L1_ffn_in['b1'], 'L1_ffn_w2': _L1_ffn_in['w2'], 'L1_ffn_b2': _L1_ffn_in['b2']}

def reference(x, L0_conv_wq, L0_conv_bq, L0_conv_wk, L0_conv_bk, L0_conv_wv, L0_conv_bv, L0_conv_gamma, L1_attn_Wk, L1_attn_Wq, L1_attn_Wv, L1_ffn_gate_w, L1_ffn_w1, L1_ffn_b1, L1_ffn_w2, L1_ffn_b2):
    import jax
    import jax.numpy as jnp

    def _L0_conv_ref(x, wq, bq, wk, bk, wv, bv, gamma):
        import jax, jax.numpy as jnp
        import numpy as np
        B, C, H, W = (4, 128, 16, 16)
        C8 = C // 8
        b, c, h, w = x.shape
        q = jnp.einsum('bchw,oc->bohw', x, wq) + bq[None, :, None, None]
        k = jnp.einsum('bchw,oc->bohw', x, wk) + bk[None, :, None, None]
        v = jnp.einsum('bchw,oc->bohw', x, wv) + bv[None, :, None, None]
        qf = q.reshape(b, c // 8, h * w)
        kf = k.reshape(b, c // 8, h * w)
        energy = jnp.einsum('bci,bcj->bij', qf, kf).reshape(b, h, w, h, w)
        attn = jax.nn.softmax(energy, axis=-1)
        out = jnp.einsum('bchk,bhwkv->bcwv', v, attn)
        return gamma * out + x

    def _L1_attn_ref(x, Wk, Wq, Wv):
        import jax, jax.numpy as jnp
        import numpy as np
        NHEAD = 8
        B, N, _ = x.shape
        H = NHEAD
        k = (x @ Wk).reshape(B, N, H, -1)
        q = (x @ Wq).reshape(B, N, H, -1)
        v = (x @ Wv).reshape(B, N, H, -1)
        dk = k.shape[-1]
        scores = jnp.einsum('bnhd,bmhd->bnmh', k, q) / jnp.sqrt(jnp.asarray(dk, x.dtype))
        attn = jax.nn.softmax(scores, axis=-2)
        out = jnp.einsum('bnmh,bmhd->bnhd', attn, v)
        return out.reshape(B, N, -1)

    def _L1_ffn_ref(x, gate_w, w1, b1, w2, b2):
        import jax, jax.numpy as jnp
        import numpy as np
        B, S, D = (8, 512, 128)
        E, K, H = (8, 2, 512)
        batch, seq, dim = x.shape
        x_flat = x.reshape(-1, dim)
        T = x_flat.shape[0]
        gate_logits = x_flat @ gate_w.T
        topk_vals, topk_idx = jax.lax.top_k(gate_logits, K)
        topk_w = jax.nn.softmax(topk_vals, axis=-1)
        comb = jnp.zeros((T, E), dtype=x_flat.dtype)
        comb = comb.at[jnp.arange(T)[:, None], topk_idx].add(topk_w)
        out = jnp.zeros_like(x_flat)
        for e in range(E):
            h = jax.nn.gelu(x_flat @ w1[e].T + b1[e], approximate=False)
            y = h @ w2[e].T + b2[e]
            out = out + comb[:, e:e + 1] * y
        return out.reshape(batch, seq, dim)

    def _gn(v, G=32, eps=1e-05):
        B_, C_, H_, W_ = v.shape
        g = v.reshape(B_, G, C_ // G, H_, W_)
        m = jnp.mean(g, axis=(2, 3, 4), keepdims=True)
        s = jnp.var(g, axis=(2, 3, 4), keepdims=True)
        return ((g - m) / jnp.sqrt(s + eps)).reshape(v.shape)

    def _ln_c(v, eps=1e-06):
        m = jnp.mean(v, axis=1, keepdims=True)
        s = jnp.var(v, axis=1, keepdims=True)
        return (v - m) / jnp.sqrt(s + eps)

    def _ln_t(v, eps=1e-05):
        m = jnp.mean(v, axis=-1, keepdims=True)
        s = jnp.var(v, axis=-1, keepdims=True)
        return (v - m) / jnp.sqrt(s + eps)

    def _to_tokens(v):
        B_, C_, H_, W_ = v.shape
        return v.reshape(B_, C_, H_ * W_).transpose(0, 2, 1)

    def _from_tokens(t, like):
        B_, C_, H_, W_ = like.shape
        return t.transpose(0, 2, 1).reshape(B_, C_, H_, W_)
    x = _L0_conv_ref(x, L0_conv_wq, L0_conv_bq, L0_conv_wk, L0_conv_bk, L0_conv_wv, L0_conv_bv, L0_conv_gamma)
    t = _to_tokens(x)
    t = t + _L1_attn_ref(_ln_t(t), L1_attn_Wk, L1_attn_Wq, L1_attn_Wv)
    t = t + _L1_ffn_ref(_ln_t(t), L1_ffn_gate_w, L1_ffn_w1, L1_ffn_b1, L1_ffn_w2, L1_ffn_b2)
    x = _from_tokens(t, x)
    return x

_drawn_inputs = setup_inputs


def setup_inputs(seed=0):
    import zlib

    import numpy as np

    out = dict(_drawn_inputs(seed))
    spreads = {}
    factors = {'L0_conv_wq': 8.0,
     'L0_conv_bq': 8.0,
     'L0_conv_wk': 8.0,
     'L0_conv_bk': 8.0,
     'L0_conv_wv': 2.861,
     'L1_ffn_b1': 8.0,
     'L1_ffn_b2': 3.92}
    for name, (base, spread) in spreads.items():
        noise = np.random.default_rng([zlib.crc32(name.encode()), seed]).standard_normal(out[name].shape)
        drawn = base * np.exp(spread * noise) if base else spread * noise
        out[name] = jnp.asarray(drawn.astype(out[name].dtype))
    for name, factor in factors.items():
        out[name] = (out[name] * factor).astype(out[name].dtype)
    return out
```

```python
import numpy as np

import concourse.bass as bass
from concourse import mybir
from concourse.alu_op_type import AluOpType as ALU
from contextlib import ExitStack

B, C, H, W = 4, 128, 16, 16
TOK = H * W
T = B * TOK
HALF = T // 2
NHALF = T // HALF
C8 = C // 8
QK = 32 + C8
HEADS, DK = 8, 16
E, HID = 8, 512
MT = HID // 128
W2N = 2
J = W // W2N
KQ, K4 = 4, 4
TILES = HALF // 128
EPS = 1e-5
BIG = 1e38
RSQRT_MAGIC = float(0x5F3759DF)

ID0, AVG0, ONE0, MASK0, RANK0, CONSTS = 0, 128, 256, 320, 323, 331


def hybrid_program(nc, x_in, x_kh_in_dram, convw, convb, bv, gamma, attw, gate, w12, b1, b2, consts, out):
    f32, f32r, i32 = mybir.dt.float32, mybir.dt.float32r, mybir.dt.int32
    ACT = mybir.ActivationFunctionType
    AX = mybir.AxisListType
    scratch = nc.dram_tensor("attn_scratch", (KQ, 128, K4 * J * W), f32, kind="Internal").ap()

    with ExitStack() as ctx:
        def sb(name, shape, dt=f32):
            return ctx.enter_context(nc.sbuf_tensor(name, shape, dt))

        def sem(name):
            return ctx.enter_context(nc.semaphore(name))

        cst = sb("cst", [128, CONSTS])
        ident, avg = cst[:, ID0:ID0 + 128], cst[:, AVG0:AVG0 + 128]
        ones_par = cst[:, ONE0:ONE0 + 64].rearrange("p (g c) -> p g c", g=2)
        lo_mask, hi_mask, row16 = (cst[:, c:c + 1] for c in (MASK0, MASK0 + 1, MASK0 + 2))
        rank = cst[:, RANK0:RANK0 + E]
        convw_sb = sb("convw_sb", [128, QK + C])
        convb_sb = sb("convb_sb", [QK, 2])
        bv_sb = sb("bv_sb", [128, C])
        gamma_sb = sb("gamma_sb", [128, 1])
        attw_sb = sb("attw_sb", [128, 5 * 128])
        gate_sb = sb("gate_sb", [128, E])
        b2_sb = sb("b2_sb", [E, 128])
        raw = [sb(f"raw{s}", [128, 2 * HID]) for s in range(2)]
        b1c = [sb(f"b1c{s}", [128, MT]) for s in range(2)]
        wst = [[sb(f"wst{s}_{n}", [128, HID], f32r) for n in ("w1h", "w1l", "w2h", "w2l")] for s in range(2)]

        x_sb = sb("x_sb", [128, T])
        t1 = sb("t1", [128, T])
        t2 = sb("t2", [128, T])
        xn = sb("xn", [128, T])
        dev = sb("dev", [128, T])
        sq = sb("sq", [128, T])

        combB = sb("combB", [128, NHALF, E, HALF])
        room = combB[:, :, :, :].rearrange("p a e t -> p (a e t)")
        A = room[:, 0:2048].rearrange("p (k j v) -> p k j v", k=W, j=J)
        S = room[:, 2048:4096].rearrange("p (q j k v) -> p q j k v", q=KQ, j=J, k=K4)
        AT = room[:, 4096:6144].rearrange("p (t n) -> p t n", t=2)
        vT = room[:, 6144:7168].rearrange("p (i c) -> p i c", c=C)
        x_kh = room[:, 7168:8192]
        cq = xn[0:C8, :]
        ck = dev[0:C8, :]
        nv, ny, na = (sb(n, [128, T // 128]) for n in ("nv", "ny", "na"))
        cmax = sb("cmax", [128, KQ, J, K4])
        csum = sb("csum", [128, KQ, K4 * J])
        crcp = sb("crcp", [128, KQ, K4 * J])

        kh = [sb(f"kh{g}", [128, T], f32r) for g in range(2)]
        kl = [sb(f"kl{g}", [128, T], f32r) for g in range(2)]
        qh = [sb(f"qh{g}", [128, HALF], f32r) for g in range(2)]
        qs = [sb(f"qs{g}", [128, T], f32r) for g in range(2)]
        q1 = [sb(f"q1{g}", [128, T], f32r) for g in range(2)]
        klm = [sb(f"klm{g}", [128, T], f32r) for g in range(2)]
        vpad = sb("vpad", [128, T // 128, HEADS, 32])
        nmx = sb("nmx", [128, 2, T // 128, 128])
        probs = sb("probs", [128, 2, 4, 2, TOK])
        G = probs[:, 0, :, :, :].rearrange("p a b c -> p a (b c)")
        rcp = sb("rcp", [128, 2, TOK])

        lg = sb("lg", [128, TILES, E])
        g_eq = sb("g_eq", [128, TILES, E])
        g_key = sb("g_key", [128, TILES, E])
        g_oh1 = sb("g_oh1", [128, TILES, E])
        g_oh2 = sb("g_oh2", [128, TILES, E])
        g_l2 = sb("g_l2", [128, TILES, E])
        comb = sb("comb", [128, NHALF, TILES, E])
        g_s = sb("g_s", [128, 8, TILES])
        combT = sb("combT", [E, T])

        x2h = sb("x2h", [128, T], f32r)
        x2l = sb("x2l", [128, T], f32r)
        hh = [sb(f"hh{i}", [128, HALF], f32r) for i in range(4)]
        hl = [sb(f"hl{i}", [128, HALF], f32r) for i in range(4)]
        part = probs[:, 1, 0:2, :, :].rearrange("p a b c -> p a (b c)")

        PS = ctx.enter_context(nc.psum_tensor("PS", [128, 8, 512], f32))

        x_in_s = [sem(f"x_in{p}") for p in range(NHALF)]
        x_kh_in, bv_in = sem("x_kh_in"), sem("bv_in")
        convw_in, attw_in, cst_in, w_in = sem("convw_in"), sem("attw_in"), sem("cst_in"), [sem(f"w_in{s}") for s in range(2)]
        whi_ready = sem("whi_ready")
        b1_in = [sem(f"b1_in{s}") for s in range(2)]
        proj_done, cq_ready, ck_ready = sem("proj_done"), sem("cq_ready"), sem("ck_ready")
        vT_done, vT_ready, energy_done = sem("vT_done"), sem("vT_ready"), sem("energy_done")
        cmax_ready, shifted, exp_ready = sem("cmax_ready"), sem("shifted"), sem("exp_ready")
        csum_ready, crcp_ready, A_ready = sem("csum_ready"), sem("crcp_ready"), sem("A_ready")
        A_out = [sem(f"A_out{i}") for i in range(KQ)]
        AT_in = [sem(f"AT_in{i}") for i in range(KQ)]
        conv_done, t1_ready = sem("conv_done"), sem("t1_ready")
        mean_done, dev_ready, sq_ready = sem("mean_done"), sem("dev_ready"), sem("sq_ready")
        var_done, spread_done, rstd_ready, xn_ready = sem("var_done"), sem("spread_done"), sem("rstd_ready"), sem("xn_ready")
        qkv_done, hi_ready, lo_ready = sem("qkv_done"), sem("hi_ready"), sem("lo_ready")
        v_done, v_ready, vzero = sem("v_done"), sem("v_ready"), sem("vzero")
        raw_done, max_ready, q1_ready = sem("raw_done"), sem("max_ready"), sem("q1_ready")
        nmT_done, nmT_ready = sem("nmT_done"), sem("nmT_ready")
        score_done, prob_ready, pv_done = sem("score_done"), sem("prob_ready"), sem("pv_done")
        rcp_ready, out_scaled, t2_ready = sem("rcp_ready"), sem("out_scaled"), sem("t2_ready")
        logits_done, x2h_ready, x2l_ready = sem("logits_done"), sem("x2h_ready"), sem("x2l_ready")
        gstep, gap_ready, gexp_ready, comb_ready = sem("gstep"), sem("gap_ready"), sem("gexp_ready"), sem("comb_ready")
        combT_done, combT_ready, bias_done, acc_ready = sem("combT_done"), sem("combT_ready"), sem("bias_done"), sem("acc_ready")
        combB_done, combB_ready = sem("combB_done"), sem("combB_ready")
        wlo_ready, up_done, gelu_done = sem("wlo_ready"), sem("up_done"), sem("gelu_done")
        hh_ready, hl_ready, down_done = sem("hh_ready"), sem("hl_ready"), sem("down_done")
        part_ready, acc_done, out_sent = sem("part_ready"), sem("acc_done"), sem("out_sent")

        block = ctx.enter_context(nc.Block())

        def cols(p):
            return slice(p * HALF, (p + 1) * HALF)

        UNITS = [(b, g) for b in range(2) for g in range(2)]
        LAG = 2
        STEPS = NHALF * MT

        NORMS = [(0, 1), (0,), (1,)]
        MEAN_BANK = [(4, 5), (4,), (4,)]
        VAR_BANK = [6, 5, 5]
        RSTD_BANK = [(7, 6), (5,), (5,)]

        @block.sync
        def _(sp):
            for p in range(NHALF):
                sp.dma_start(x_sb[:, cols(p)], x_in[:, cols(p)]).then_inc(x_in_s[p], 16)
            sp.dma_start(x_kh[:, :], x_kh_in_dram).then_inc(x_kh_in, 16)
            sp.dma_start(attw_sb[:, :], attw).then_inc(attw_in, 16)
            def expert_weights(e, s):
                if not (isinstance(e, int) and e < 2):
                    sp.wait_ge(wlo_ready, 2 * (e - 1))
                sp.dma_start(raw[s][:, :], w12[bass.ds(e, 1), :, :].rearrange("a p n -> (a p) n")).then_inc(w_in[s], 16)

            def expert_bias(e, s):
                if not (isinstance(e, int) and e < 2):
                    sp.wait_ge(gelu_done, STEPS * (e - 1))
                sp.dma_start(b1c[s][:, :], b1[bass.ds(e, 1), :, :].rearrange("a p n -> (a p) n")).then_inc(b1_in[s], 16)

            for e in range(2):
                expert_weights(e, e)
                expert_bias(e, e)
            for q in range(KQ):
                sp.wait_ge(A_ready, q + 1)
                sp.dma_start(scratch[q], A[:, q * K4:(q + 1) * K4, :, :].rearrange("p k j v -> p (k j v)"))\
                    .then_inc(A_out[q], 16)
            for q in range(KQ):
                sp.wait_ge(A_out[q], 16)
                src = scratch[q].rearrange("(bw h) (k r) -> (h k) bw r", h=H, k=K4)
                dst = AT[64 * (q % 2):64 * (q % 2) + 64, q // 2, :].rearrange("p (bw r) -> p bw r", bw=2 * B)
                sp.dma_start(dst, src).then_inc(AT_in[q], 16)
            with sp.Fori(1, E // 2) as i:
                for s in range(2):
                    expert_weights(2 * i + s, s)
                    expert_bias(2 * i + s, s)
            for p in range(NHALF):
                sp.wait_ge(acc_done, NHALF * (E - 1) + p + 1)
                sp.dma_start(out[:, cols(p)], t2[:, cols(p)]).then_inc(out_sent, 16)
            sp.wait_ge(out_sent, 16 * NHALF)

        @block.gpsimd
        def _(pool):
            nc.gpsimd.memset(vpad[:, :, :, :], 0.0).then_inc(vzero, 1)
            nc.gpsimd.memset(nmx[:, :, :, :], 0.0).then_inc(vzero, 1)
            for q in range(KQ):
                pool.wait_ge(crcp_ready, q + 1)
                a = A[:, q * K4:(q + 1) * K4, :, :].rearrange("p k j v -> p (k j) v")
                nc.gpsimd.tensor_tensor(a, a, crcp[:, q, :].unsqueeze(2).broadcast_to([128, K4 * J, W]), ALU.mult)\
                    .then_inc(A_ready, 1)

            def low_weights(i, s):
                for n in range(2):
                    pool.wait_ge(whi_ready, 2 * (2 * i + s) + n + 1)
                    nc.gpsimd.tensor_tensor(wst[s][2 * n + 1][:, :], raw[s][:, n * HID:(n + 1) * HID],
                                            wst[s][2 * n][:, :].bitcast(f32), ALU.subtract).then_inc(wlo_ready, 1)

            low_weights(0, 0)
            low_weights(0, 1)
            pool.wait_ge(acc_ready, NHALF)

            def expert_pair(i, last):
                for s in range(2):
                    e = 2 * i + s
                    for p in range(NHALF):
                        pool.wait_ge(part_ready, NHALF * e + p + 1)
                        nc.gpsimd.tensor_tensor(t2[:, cols(p)], t2[:, cols(p)], part[:, p, :], ALU.add)\
                            .then_inc(acc_done, 1)
                    if not last:
                        low_weights(i + 1, s)

            with pool.Fori(0, E // 2 - 1) as i:
                expert_pair(i, False)
            expert_pair(E // 2 - 1, True)

        @block.scalar
        def _(act):
            act.dma_start(convw_sb[:, :], convw).then_inc(convw_in, 16)
            act.dma_start(convb_sb[:, :], convb).then_inc(convw_in, 16)
            act.dma_start(bv_sb[:, :], bv.partition_broadcast(128)).then_inc(bv_in, 16)
            act.dma_start(gamma_sb[:, :], gamma.partition_broadcast(128)).then_inc(bv_in, 16)
            act.dma_start(cst[:, :], consts).then_inc(cst_in, 16)
            act.dma_start(gate_sb[:, :], gate).then_inc(cst_in, 16)
            act.dma_start(b2_sb[:, :], b2).then_inc(cst_in, 16)
            act.wait_ge(convw_in, 32)
            for p in range(NHALF):
                act.wait_ge(proj_done, p + 1)
                for b in range(2):
                    nc.scalar.activation(
                        cq[:, (2 * p + b) * TOK:(2 * p + b + 1) * TOK].rearrange("c (j w h) -> c h w j", j=J, w=W2N),
                        PS[0:C8, p, b * TOK:(b + 1) * TOK].rearrange("c (h w j) -> c h w j", h=H, w=W2N),
                        ACT.Identity, bias=convb_sb[0:C8, 0:1]).then_inc(cq_ready, 1)
            for q in range(KQ):
                act.wait_ge(shifted, q + 1)
                nc.scalar.activation(A[:, q * K4:(q + 1) * K4, :, :].rearrange("p k j v -> p j k v"), S[:, q],
                                     ACT.Exp).then_inc(exp_ready, 1)
            act.wait_ge(cst_in, 48)

            def norm_square(n):
                for i, p in enumerate(NORMS[n]):
                    act.wait_ge(dev_ready, n + i + (n > 0) + 1)
                    nc.scalar.activation(sq[:, cols(p)], dev[:, cols(p)], ACT.Square).then_inc(sq_ready, 1)

            def high_weights(i, s):
                act.wait_ge(w_in[s], 16 * i + 16)
                if not (isinstance(i, int) and i == 0):
                    act.wait_ge(down_done, STEPS * (2 * i + s - 1))
                for n in range(2):
                    nc.scalar.activation(wst[s][2 * n][:, :], raw[s][:, n * HID:(n + 1) * HID], ACT.Copy)\
                        .then_inc(whi_ready, 1)

            high_weights(0, 0)
            high_weights(0, 1)
            norm_square(0)

            def high_parts(p):
                for g in range(2):
                    act.wait_ge(qkv_done, 4 * p + g + 1)
                    nc.scalar.activation(kh[g][:, cols(p)], PS[:, g, :], ACT.Copy).then_inc(hi_ready, 1)
                for g in range(2):
                    act.wait_ge(qkv_done, 4 * p + 2 + g + 1)
                    if p:
                        act.wait_ge(lo_ready, 4 * p - 2 + g + 1)
                    nc.scalar.activation(qh[g][:, :], PS[:, 2 + g, :], ACT.Copy).then_inc(hi_ready, 1)
                    nc.scalar.activation(q1[g][:, cols(p)], PS[:, 2 + g, :], ACT.Identity, scale=hi_mask,
                                         bias=row16).then_inc(q1_ready, 1)

            high_parts(0)
            high_parts(1)

            def exps(u):
                for s in range(2):
                    act.wait_ge(score_done, 2 * u + s + 1)
                    if u >= 2:
                        act.wait_ge(pv_done, u - 1)
                    nc.scalar.activation(probs[:, u % 2, 2 * s:2 * s + 2, :, :].rearrange("p a b c -> p (a b c)"),
                                         PS[:, 2 * s:2 * s + 2, :].rearrange("p a b -> p (a b)"), ACT.Exp,
                                         scale=DK ** -0.5).then_inc(prob_ready, 1)

            def gate_exp(p):
                act.wait_ge(gap_ready, p + 1)
                nc.scalar.activation(g_s[:, 4, :], g_s[:, 3, :], ACT.Exp).then_inc(gexp_ready, 1)

            def combs(p):
                for e in range(E):
                    n = p * E + e
                    act.wait_ge(combB_done, n + 1)
                    nc.scalar.activation(combB[:, p, e, :], PS[:, 4 + e % 2, :], ACT.Copy).then_inc(combB_ready, 1)

            for u in range(8):
                exps(u)
                if u == 5:
                    norm_square(1)
                if u == 7:
                    gate_exp(0)
                    combs(0)
            norm_square(2)
            gate_exp(1)
            combs(1)

            def gelu(i, s):
                n = 2 * STEPS * i + s
                act.wait_ge(up_done, n + 1)
                if not (isinstance(i, int) and n < 4):
                    act.wait_ge(hl_ready, n - 3)
                if s % STEPS == 0:
                    act.wait_ge(b1_in[s // STEPS], 16 * i + 16)
                nc.scalar.activation(G[:, s % 4, :], PS[:, s % 4, :], ACT.Gelu,
                                     bias=b1c[s // STEPS][:, s % MT:s % MT + 1]).then_inc(gelu_done, 1)

            def gelus(i, last):
                for s in range(2 * STEPS):
                    gelu(i, s)
                    if s == STEPS + 4 and not last:
                        high_weights(i + 1, 0)
                    if s == 4 and not (isinstance(i, int) and i == 0):
                        high_weights(i, 1)

            gelus(0, False)
            with act.Fori(1, E // 2 - 1) as i:
                gelus(i, False)
            gelus(E // 2 - 1, True)

        @block.vector
        def _(dve):
            dve.wait_ge(convw_in, 32)
            for p in range(NHALF):
                dve.wait_ge(proj_done, p + 1)
                nc.vector.tensor_scalar(ck[:, cols(p)], PS[32:QK, p, :], convb_sb[32:QK, 1:2], None, ALU.add)\
                    .then_inc(ck_ready, 1)
            dve.wait_ge(bv_in, 32)
            for i in range(2):
                dve.wait_ge(vT_done, i + 1)
                nc.vector.tensor_tensor(vT[:, 4 * i:4 * i + 4, :],
                                        PS[:, 4 + i, :].rearrange("p (a c) -> p a c", c=C),
                                        bv_sb[:, :].unsqueeze(1).broadcast_to([128, 4, C]), ALU.add).then_inc(vT_ready, 1)
            dve.wait_ge(energy_done, 1)
            En = PS[:, 0:4, :].rearrange("p a b -> p (a b)").rearrange("p (j k v) -> p j k v", j=J, k=W)

            def shift(q):
                e = En[:, :, q * K4:(q + 1) * K4, :]
                nc.vector.tensor_reduce(cmax[:, q], e, AX.X, ALU.max).then_inc(cmax_ready, 1)
                dve.wait_ge(cmax_ready, q + 1)
                nc.vector.tensor_tensor(S[:, q], e, cmax[:, q].unsqueeze(3).broadcast_to([128, J, K4, W]),
                                        ALU.subtract).then_inc(shifted, 1)

            def sums(q):
                dve.wait_ge(exp_ready, q + 1)
                nc.vector.tensor_reduce(csum[:, q], A[:, q * K4:(q + 1) * K4, :, :].rearrange("p k j v -> p (k j) v"),
                                        AX.X, ALU.add).then_inc(csum_ready, 1)
                dve.wait_ge(csum_ready, q + 1)
                nc.vector.reciprocal(crcp[:, q], csum[:, q]).then_inc(crcp_ready, 1)

            shift(0)
            for q in range(1, KQ):
                shift(q)
                sums(q - 1)
            sums(KQ - 1)
            dve.wait_ge(cst_in, 48)
            for p in range(NHALF):
                dve.wait_ge(conv_done, p + 1)
                if p == 0:
                    for q in range(NHALF):
                        dve.wait_ge(x_in_s[q], 16)
                nc.vector.scalar_tensor_tensor(
                    t1[:, cols(p)].rearrange("p (b n) -> p b n", b=2), PS[:, 4 + 2 * p:6 + 2 * p, 0:TOK],
                    gamma_sb[:, 0:1], x_sb[:, cols(p)].rearrange("p (b n) -> p b n", b=2),
                    ALU.mult, ALU.add).then_inc(t1_ready, 1)

            steps = [0]

            def then(ins):
                steps[0] += 1
                ins.then_inc(gstep, 1)
                dve.wait_ge(gstep, steps[0])

            def norm_dev(n):
                src = t1 if n == 0 else t2
                for i, p in enumerate(NORMS[n]):
                    dve.wait_ge(mean_done, n + i + (n > 0) + 1)
                    nc.vector.tensor_tensor(dev[:, cols(p)], src[:, cols(p)], PS[:, MEAN_BANK[n][i], :],
                                            ALU.subtract).then_inc(dev_ready, 1)

            def norm_rstd(n):
                w = TILES * len(NORMS[n])
                v, y, a = nv[:, 0:w], ny[:, 0:w], na[:, 0:w]
                dve.wait_ge(var_done, n + 1)
                then(nc.vector.tensor_scalar(v, PS[:, VAR_BANK[n], 0:w], EPS, None, ALU.add))
                then(nc.vector.tensor_scalar(a.bitcast(i32), v.bitcast(i32), 1, None, ALU.logical_shift_right))
                then(nc.vector.tensor_scalar(y.bitcast(i32), a.bitcast(i32), -1.0, RSQRT_MAGIC, ALU.mult, ALU.add))
                then(nc.vector.tensor_scalar(v, v, -0.5, None, ALU.mult))
                for k in range(3):
                    then(nc.vector.tensor_tensor(a, y, y, ALU.mult))
                    then(nc.vector.tensor_tensor(a, a, v, ALU.mult))
                    last = nc.vector.scalar_tensor_tensor(y, a, 1.5, y, ALU.add, ALU.mult)
                    if k < 2:
                        then(last)
                last.then_inc(rstd_ready, 1)

            def norm_out(n):
                for i, p in enumerate(NORMS[n]):
                    dve.wait_ge(spread_done, n + i + (n > 0) + 1)
                    nc.vector.tensor_tensor(xn[:, cols(p)], dev[:, cols(p)], PS[:, RSTD_BANK[n][i], :],
                                            ALU.mult).then_inc(xn_ready, 1)

            norm_dev(0)
            norm_rstd(0)
            norm_out(0)

            def low_parts(p):
                for g in range(2):
                    dve.wait_ge(hi_ready, 4 * p + g + 1)
                    nc.vector.tensor_tensor(kl[g][:, cols(p)], PS[:, g, :], kh[g][:, cols(p)].bitcast(f32),
                                            ALU.subtract).then_inc(lo_ready, 1)
                for g in range(2):
                    dve.wait_ge(hi_ready, 4 * p + 2 + g + 1)
                    dve.wait_ge(q1_ready, 2 * p + g + 1)
                    nc.vector.scalar_tensor_tensor(qs[g][:, cols(p)], qh[g][:, :].bitcast(f32), lo_mask,
                                                   PS[:, 2 + g, :], ALU.mult, ALU.add).then_inc(lo_ready, 1)

            def values(p):
                dve.wait_ge(v_done, p + 1)
                dst = vpad[:, TILES * p:TILES * (p + 1), :, :].rearrange("p t h c -> p (t h c)")\
                    .rearrange("p (th r) -> p th r", r=64)
                src = PS[:, 4 + p, :].rearrange("p (th r) -> p th r", r=32)
                for par in range(2):
                    nc.vector.tensor_copy(dst[:, :, 48 * par:48 * par + DK], src[:, :, DK * par:DK * (par + 1)])\
                        .then_inc(v_ready, 1)

            low_parts(0)
            dve.wait_ge(vzero, 2)
            values(0)
            low_parts(1)
            values(1)

            def raw_max(t):
                for s in range(4):
                    n = 4 * t + s
                    dve.wait_ge(raw_done, n + 1)
                    nc.vector.tensor_reduce(nmx[:, :, t, 32 * s + DK],
                                            PS[:, 4 + n % 2, :].rearrange("p (a m) -> p a m", a=2), AX.X, ALU.max,
                                            negate=True).then_inc(max_ready, 1)

            def max_rows(p):
                for g in range(2):
                    dve.wait_ge(nmT_done, 2 * p + g + 1)
                    nc.vector.tensor_tensor(klm[g][:, cols(p)], kl[g][:, cols(p)].bitcast(f32), PS[:, 4 + g, :],
                                            ALU.add).then_inc(nmT_ready, 1)

            def attend(b):
                tok = slice(b * TOK, (b + 1) * TOK)
                dve.wait_ge(pv_done, 2 * (b + 1))
                if b >= 2:
                    dve.wait_ge(t2_ready, b - 1)
                nc.vector.reciprocal(rcp[:, b % 2, :], PS[:, 6 + b % 2, TOK:2 * TOK]).then_inc(rcp_ready, 1)
                dve.wait_ge(rcp_ready, b + 1)
                nc.vector.tensor_tensor(rcp[:, b % 2, :], PS[:, 6 + b % 2, 0:TOK], rcp[:, b % 2, :], ALU.mult).then_inc(out_scaled, 1)
                dve.wait_ge(out_scaled, b + 1)
                nc.vector.tensor_tensor(t2[:, tok], t1[:, tok], rcp[:, b % 2, :], ALU.add).then_inc(t2_ready, 1)

            def split_x2(p):
                dve.wait_ge(xn_ready, NHALF + p + 1)
                nc.vector.tensor_copy(x2h[:, cols(p)], xn[:, cols(p)]).then_inc(x2h_ready, 1)
                dve.wait_ge(x2h_ready, p + 1)
                nc.vector.tensor_tensor(x2l[:, cols(p)], xn[:, cols(p)], x2h[:, cols(p)].bitcast(f32), ALU.subtract)\
                    .then_inc(x2l_ready, 1)

            def spread(v):
                return v.unsqueeze(2).broadcast_to([128, TILES, E])

            def first_of(logits, top, onehot):
                then(nc.vector.tensor_reduce(top, logits, AX.X, ALU.max))
                then(nc.vector.tensor_tensor(g_eq[:, :, :], logits, spread(top), ALU.is_equal))
                then(nc.vector.tensor_tensor(g_key[:, :, :], g_eq[:, :, :],
                                             rank.unsqueeze(1).broadcast_to([128, TILES, E]), ALU.mult))
                then(nc.vector.tensor_reduce(g_s[:, 2, :], g_key[:, :, :], AX.X, ALU.max))
                then(nc.vector.tensor_tensor(onehot, g_key[:, :, :], spread(g_s[:, 2, :]), ALU.is_equal))

            def top_two(p):
                dve.wait_ge(logits_done, p + 1)
                then(nc.vector.tensor_copy(lg[:, :, :].rearrange("p t e -> p (t e)"), PS[:, 4, 0:TILES * E]))
                first_of(lg[:, :, :], g_s[:, 0, :], g_oh1[:, :, :])
                then(nc.vector.scalar_tensor_tensor(g_l2[:, :, :], g_oh1[:, :, :], -BIG, lg[:, :, :], ALU.mult, ALU.add))
                first_of(g_l2[:, :, :], g_s[:, 1, :], g_oh2[:, :, :])
                nc.vector.tensor_tensor(g_s[:, 3, :], g_s[:, 1, :], g_s[:, 0, :], ALU.subtract).then_inc(gap_ready, 1)
                dve.wait_ge(gexp_ready, p + 1)
                then(nc.vector.tensor_scalar(g_s[:, 5, :], g_s[:, 4, :], 1.0, None, ALU.add))
                then(nc.vector.reciprocal(g_s[:, 6, :], g_s[:, 5, :]))
                then(nc.vector.tensor_tensor(g_s[:, 7, :], g_s[:, 4, :], g_s[:, 6, :], ALU.mult))
                then(nc.vector.tensor_tensor(g_oh1[:, :, :], g_oh1[:, :, :], spread(g_s[:, 6, :]), ALU.mult))
                then(nc.vector.tensor_tensor(g_oh2[:, :, :], g_oh2[:, :, :], spread(g_s[:, 7, :]), ALU.mult))
                nc.vector.tensor_tensor(comb[:, p], g_oh1[:, :, :], g_oh2[:, :, :], ALU.add).then_inc(comb_ready, 1)

            def bias_sum(p):
                dve.wait_ge(combT_done, p + 1)
                nc.vector.tensor_copy(combT[:, cols(p)], PS[0:E, 5, :]).then_inc(combT_ready, 1)
                dve.wait_ge(bias_done, p + 1)
                nc.vector.tensor_tensor(t2[:, cols(p)], t2[:, cols(p)], PS[:, 4, :], ALU.add).then_inc(acc_ready, 1)

            for t in range(TILES):
                raw_max(t)
            max_rows(0)
            for t in range(TILES):
                raw_max(TILES + t)
            max_rows(1)
            attend(0)
            attend(1)
            norm_dev(1)
            norm_rstd(1)
            norm_out(1)
            split_x2(0)
            top_two(0)
            bias_sum(0)
            attend(2)
            attend(3)
            norm_dev(2)
            norm_rstd(2)
            norm_out(2)
            split_x2(1)
            top_two(1)
            bias_sum(1)

            def parts(i, s):
                n = 2 * STEPS * i + s
                b = s % 4
                dve.wait_ge(gelu_done, n + 1)
                if not (isinstance(i, int) and n < 4):
                    dve.wait_ge(down_done, n - 3)
                nc.vector.tensor_copy(hh[b][:, :], G[:, b, :]).then_inc(hh_ready, 1)
                dve.wait_ge(hh_ready, n + 1)
                nc.vector.tensor_tensor(hl[b][:, :], G[:, b, :], hh[b][:, :].bitcast(f32), ALU.subtract)\
                    .then_inc(hl_ready, 1)

            def weigh(i, r):
                p, e, n = r % NHALF, 2 * i + r // NHALF, 2 * NHALF * i + r
                dve.wait_ge(down_done, MT * (n + 1))
                if not (isinstance(i, int) and n < NHALF):
                    dve.wait_ge(acc_done, n - 1)
                nc.vector.tensor_tensor(part[:, p, :], PS[:, 6 + p, :], combB[:, p, bass.ds(e, 1), :]
                                        .rearrange("p a t -> p (a t)"), ALU.mult).then_inc(part_ready, 1)

            AHEAD = 3
            for p in range(NHALF):
                dve.wait_ge(combB_ready, E * (p + 1))
            for s in range(AHEAD):
                parts(0, s)

            def expert_pair(i, last):
                for s in range(2 * STEPS):
                    if not (last and s + AHEAD >= 2 * STEPS):
                        parts(i, s + AHEAD)
                    if s % MT == MT - 1:
                        weigh(i, s // MT)

            expert_pair(0, False)
            with dve.Fori(1, E // 2 - 1) as i:
                expert_pair(i, False)
            expert_pair(E // 2 - 1, True)

        @block.tensor
        def _(pe):
            mm = nc.tensor.matmul
            pe.wait_ge(convw_in, 32)
            for p in range(NHALF):
                pe.wait_ge(x_in_s[p], 16)
                mm(PS[0:QK, p, :], convw_sb[:, 0:QK], x_sb[:, cols(p)], start=True, stop=True).then_inc(proj_done, 1)
            pe.wait_ge(x_kh_in, 16)
            for b in range(B):
                for kt in range(2):
                    i = 2 * b + kt
                    toks = x_kh[:, i * 128:(i + 1) * 128]
                    last = mm(PS[:, 4 + i // 4, (i % 4) * C:(i % 4 + 1) * C], toks, convw_sb[:, QK:QK + C],
                              start=True, stop=True)
                if b % 2:
                    last.then_inc(vT_done, 1)
            pe.wait_ge(cq_ready, B)
            pe.wait_ge(ck_ready, NHALF)
            for j in range(J):
                for b in range(B):
                    rows = cq[:, b * TOK + j * 32:b * TOK + (j + 1) * 32]
                    last = mm(PS[32 * b:32 * (b + 1), j // 2, (j % 2) * TOK:(j % 2 + 1) * TOK], rows,
                              ck[:, b * TOK:(b + 1) * TOK], start=True, stop=True)
            last.then_inc(energy_done, 1)
            pe.wait_ge(vT_ready, 2)
            for kt in range(2):
                pe.wait_ge(AT_in[2 * kt], 16)
                pe.wait_ge(AT_in[2 * kt + 1], 16)
                for b in range(B):
                    last = mm(PS[:, 4 + b, 0:TOK], vT[:, 2 * b + kt, :], AT[:, kt, b * TOK:(b + 1) * TOK],
                              start=(kt == 0), stop=(kt == 1))
                    if kt and b % 2:
                        last.then_inc(conv_done, 1)

            def norm_mean(n):
                src = t1 if n == 0 else t2
                for i, p in enumerate(NORMS[n]):
                    pe.wait_ge(t2_ready if n else t1_ready, 2 * (p + 1) if n else p + 1)
                    if n == 2:
                        pe.wait_ge(combB_ready, E)
                    mm(PS[:, MEAN_BANK[n][i], :], avg, src[:, cols(p)], start=True, stop=True).then_inc(mean_done, 1)

            def norm_var(n):
                for i, p in enumerate(NORMS[n]):
                    pe.wait_ge(sq_ready, n + i + (n > 0) + 1)
                    for t in range(TILES):
                        last = mm(PS[:, VAR_BANK[n], TILES * i + t:TILES * i + t + 1],
                                  sq[:, p * HALF + t * 128:p * HALF + (t + 1) * 128], avg[:, 0:1], start=True, stop=True)
                last.then_inc(var_done, 1)

            def norm_spread(n):
                pe.wait_ge(rstd_ready, n + 1)
                for i, p in enumerate(NORMS[n]):
                    for t in range(TILES):
                        c = TILES * i + t
                        last = nc.tensor.transpose(PS[:, RSTD_BANK[n][i], t * 128:(t + 1) * 128],
                                                   ny[:, c:c + 1].broadcast_to([128, 128]), ident)
                    last.then_inc(spread_done, 1)

            pe.wait_ge(cst_in, 48)
            norm_mean(0)
            norm_var(0)
            norm_spread(0)
            pe.wait_ge(attw_in, 16)

            def project(p):
                pe.wait_ge(xn_ready, p + 1)
                if p:
                    pe.wait_ge(lo_ready, 4)
                for n in range(4):
                    mm(PS[:, n, :], attw_sb[:, n * 128:(n + 1) * 128], xn[:, cols(p)], start=True, stop=True)\
                        .then_inc(qkv_done, 1)
                for t in range(TILES):
                    last = mm(PS[:, 4 + p, t * 128:(t + 1) * 128], xn[:, p * HALF + t * 128:p * HALF + (t + 1) * 128],
                              attw_sb[:, 512:640], start=True, stop=True)
                last.then_inc(v_done, 1)

            project(0)
            project(1)

            def head_rows(j):
                return slice(32 * j, 32 * j + 32)

            def raw_scores(t):
                if t == 0:
                    pe.wait_ge(lo_ready, 8)
                    pe.wait_ge(v_ready, 4)
                b = t // 2
                for s in range(4):
                    n = 4 * t + s
                    if n >= 2:
                        pe.wait_ge(max_ready, n - 1)
                    if n == 4 * TILES:
                        pe.wait_ge(nmT_ready, 2)
                    for g in range(2):
                        last = mm(PS[:, 4 + n % 2, g * TOK:(g + 1) * TOK], kh[g][head_rows(s), t * 128:(t + 1) * 128],
                                  qs[g][head_rows(s), b * TOK:(b + 1) * TOK], start=True, stop=True)
                    last.then_inc(raw_done, 1)

            def max_transpose(p):
                pe.wait_ge(max_ready, 16 * (p + 1))
                for g in range(2):
                    for t in range(TILES):
                        last = nc.tensor.transpose(PS[:, 4 + g, t * 128:(t + 1) * 128], nmx[:, g, TILES * p + t, :],
                                                   ident)
                    last.then_inc(nmT_done, 1)

            def scores(u):
                b, g = u // 2, u % 2
                pe.wait_ge(nmT_ready, 2 * (b // 2) + g + 1)
                tok = slice(b * TOK, (b + 1) * TOK)
                for s in range(2):
                    if u:
                        pe.wait_ge(prob_ready, 2 * (u - 1) + s + 1)
                    for a in range(2):
                        j = 2 * s + a
                        for mt in range(2):
                            o = PS[:, j, mt * TOK:(mt + 1) * TOK]
                            m = slice(b * TOK + mt * 128, b * TOK + (mt + 1) * 128)
                            mm(o, qs[g][head_rows(j), m], kh[g][head_rows(j), tok], start=True, stop=False)
                            last = mm(o, q1[g][head_rows(j), m], klm[g][head_rows(j), tok], start=False, stop=True)
                    last.then_inc(score_done, 1)

            def attend(u):
                b, g = u // 2, u % 2
                if u >= 4:
                    pe.wait_ge(t2_ready, b - 1)
                pe.wait_ge(prob_ready, 2 * u + 2)
                for out_part in (True, False):
                    for mt in range(2):
                        for j in range(4):
                            wt = vpad[:, 2 * b + mt, 2 * j + g, :] if out_part else ones_par[:, g, :]
                            o = PS[head_rows(j), 6 + b % 2, 0:TOK] if out_part else \
                                PS[head_rows(j), 6 + b % 2, TOK:2 * TOK]
                            last = mm(o, wt, probs[:, u % 2, j, mt, :], start=(out_part and g == 0 and mt == 0),
                                      stop=(g == 1 and mt == 1), skip_group_check=True)
                last.then_inc(pv_done, 1)

            def logits(p):
                pe.wait_ge(xn_ready, NHALF + p + 1)
                for t in range(TILES):
                    last = mm(PS[:, 4, t * E:(t + 1) * E], xn[:, p * HALF + t * 128:p * HALF + (t + 1) * 128],
                              gate_sb[:, :], start=True, stop=True)
                last.then_inc(logits_done, 1)

            def comb_rows(p):
                pe.wait_ge(comb_ready, p + 1)
                for t in range(TILES):
                    last = nc.tensor.transpose(PS[0:E, 5, t * 128:(t + 1) * 128], comb[:, p, t, :], ident)
                last.then_inc(combT_done, 1)
                pe.wait_ge(combT_ready, p + 1)
                mm(PS[:, 4, :], b2_sb[:, :], combT[:, cols(p)], start=True, stop=True).then_inc(bias_done, 1)

            def comb_spread(p):
                for e in range(E):
                    n = p * E + e
                    if e < 2:
                        pe.wait_ge(acc_ready, p + 1)
                    else:
                        pe.wait_ge(combB_ready, n - 1)
                    for t in range(TILES):
                        last = nc.tensor.transpose(PS[:, 4 + e % 2, t * 128:(t + 1) * 128],
                                                   comb[:, p, t, e:e + 1].broadcast_to([128, 128]), ident)
                    last.then_inc(combB_done, 1)

            for t in range(TILES):
                raw_scores(t)
            max_transpose(0)
            scores(0)
            for u in range(8):
                if u < TILES:
                    raw_scores(TILES + u)
                if u == 3:
                    max_transpose(1)
                if u + 1 < 8:
                    scores(u + 1)
                attend(u)
                if u == 5:
                    norm_mean(1)
                if u == 6:
                    norm_var(1)
                    norm_spread(1)
                if u == 7:
                    logits(0)
                    comb_rows(0)
                    comb_spread(0)
            norm_mean(2)
            norm_var(2)
            norm_spread(2)
            logits(1)
            comb_rows(1)
            comb_spread(1)

            def up(i, s):
                n = 2 * STEPS * i + s
                w, p, m = wst[s // STEPS % 2], s % STEPS // MT, s % MT
                if s % STEPS == 0:
                    pe.wait_ge(wlo_ready, 4 * i + 2 * (s // STEPS) + 2)
                if not (isinstance(i, int) and n < 4):
                    pe.wait_ge(gelu_done, n - 3)
                o, ms = PS[:, s % 4, :], slice(m * 128, (m + 1) * 128)
                mm(o, w[0][:, ms], x2h[:, cols(p)], start=True, stop=False)
                mm(o, w[0][:, ms], x2l[:, cols(p)], start=False, stop=False)
                mm(o, w[1][:, ms], x2h[:, cols(p)], start=False, stop=True).then_inc(up_done, 1)

            def down(i, s):
                n = 2 * STEPS * i + s
                w, p, m = wst[s // STEPS], s % STEPS // MT, s % MT
                r = 2 * NHALF * i + s // MT
                if m == 0 and not (isinstance(i, int) and r < NHALF):
                    pe.wait_ge(part_ready, r - 1)
                pe.wait_ge(hl_ready, n + 1)
                o, ms = PS[:, 6 + p, :], slice(m * 128, (m + 1) * 128)
                mm(o, w[2][:, ms], hh[s % 4][:, :], start=(m == 0), stop=False)
                mm(o, w[3][:, ms], hh[s % 4][:, :], start=False, stop=False)
                mm(o, w[2][:, ms], hl[s % 4][:, :], start=False, stop=(m == MT - 1)).then_inc(down_done, 1)

            pe.wait_ge(x2l_ready, NHALF)
            for s in range(LAG):
                up(0, s)

            def expert_pair(i, last):
                for s in range(2 * STEPS):
                    if not (last and s + LAG >= 2 * STEPS):
                        up(i, s + LAG)
                    down(i, s)

            expert_pair(0, False)
            with pe.Fori(1, E // 2 - 1) as i:
                expert_pair(i, False)
            expert_pair(E // 2 - 1, True)


def kernel(**inputs):
    import concourse.bacc as bacc
    from concourse.bass_utils import run_bass_kernel_spmd

    a = {k: np.asarray(v) for k, v in inputs.items()}

    def by_parity(w):
        w = w.reshape(C, HEADS // 2, 2, 1, DK).transpose(0, 2, 1, 3, 4)
        return np.broadcast_to(w, (C, 2, HEADS // 2, 2, DK)).reshape(C, 256)

    consts = np.zeros((128, CONSTS), np.float32)
    consts[:, ID0:ID0 + 128] = np.eye(128)
    consts[:, AVG0:AVG0 + 128] = 1.0 / C
    consts[:, ONE0:ONE0 + DK] = 1.0
    consts[:, ONE0 + 32 + DK:ONE0 + 64] = 1.0
    consts[:, MASK0] = np.where(np.arange(128) % 32 < DK, 0.0, -1.0)
    consts[:, MASK0 + 1] = np.arange(128) % 32 < DK
    consts[:, MASK0 + 2] = np.arange(128) % 32 == DK
    consts[:, RANK0:RANK0 + E] = E - np.arange(E)

    arrays = {
        "x": a["x"].reshape(B, C, TOK).transpose(1, 0, 2).reshape(C, T),
        "x_kh": a["x"].reshape(B, C, H, KQ, K4).transpose(1, 0, 3, 2, 4).reshape(C, T),
        "convw": np.concatenate([a["L0_conv_wq"].T, np.zeros((C, 32 - C8), np.float32), a["L0_conv_wk"].T,
                                 a["L0_conv_wv"].T], axis=1),
        "convb": np.stack([np.pad(a["L0_conv_bq"], (0, 32)), np.pad(a["L0_conv_bk"], (32, 0))], axis=1),
        "bv": a["L0_conv_bv"],
        "gamma": a["L0_conv_gamma"],
        "attw": np.concatenate([by_parity(a["L1_attn_Wk"]), by_parity(a["L1_attn_Wq"]), a["L1_attn_Wv"]], axis=1),
        "gate": a["L1_ffn_gate_w"].T,
        "w12": np.concatenate([a["L1_ffn_w1"].transpose(0, 2, 1),
                               a["L1_ffn_w2"].reshape(E, C, MT, 128).transpose(0, 3, 2, 1).reshape(E, 128, HID)],
                              axis=2),
        "b1": a["L1_ffn_b1"].reshape(E, MT, 128).transpose(0, 2, 1),
        "b2": a["L1_ffn_b2"],
        "consts": consts,
    }
    arrays = {k: np.ascontiguousarray(v) for k, v in arrays.items()}
    nc = bacc.Bacc("TRN2", target_bir_lowering=False, num_devices=1)
    args = [nc.dram_tensor(k, v.shape, mybir.dt.from_np(v.dtype), kind="ExternalInput").ap()
            for k, v in arrays.items()]
    out = nc.dram_tensor("out", (C, T), mybir.dt.float32, kind="ExternalOutput").ap()
    hybrid_program(nc, *args, out)
    r = run_bass_kernel_spmd(nc, [arrays], core_ids=[0])
    return r.results[0]["out"].reshape(C, B, H, W).transpose(1, 0, 2, 3)
```

```python
import numpy as np

import concourse.bass as bass
from concourse import mybir
from concourse.alu_op_type import AluOpType as ALU
from contextlib import ExitStack

B, C, H, W = 4, 128, 16, 16
TOK = H * W
T = B * TOK
HALF = T // 2
NHALF = T // HALF
C8 = C // 8
QK = 32 + C8
HEADS, DK = 8, 16
E, HID = 8, 512
MT = HID // 128
W2N = 2
J = W // W2N
KQ, K4 = 4, 4
TILES = HALF // 128
EPS = 1e-5
GR, HR = 4, 4
BIG = 1e38
RSQRT_MAGIC = float(0x5F3759DF - (1 << 22))

ID0, AVG0, ONE0, MASK0, INDEX0, CONSTS = 0, 128, 256, 320, 323, 331


def hybrid_program(nc, x_in, x_kh_in_dram, convw, convb, bv, gamma, attw, gate, w12, b1, b2, consts, out):
    f32, f32r, i32 = mybir.dt.float32, mybir.dt.float32r, mybir.dt.int32
    ACT = mybir.ActivationFunctionType
    AX = mybir.AxisListType
    scratch = nc.dram_tensor("attn_scratch", (KQ, 128, K4 * J * W), f32, kind="Internal").ap()

    with ExitStack() as ctx:
        def sb(name, shape, dt=f32):
            return ctx.enter_context(nc.sbuf_tensor(name, shape, dt))

        def sem(name):
            return ctx.enter_context(nc.semaphore(name))

        cst = sb("cst", [128, CONSTS])
        ident, avg = cst[:, ID0:ID0 + 128], cst[:, AVG0:AVG0 + 128]
        ones_par = cst[:, ONE0:ONE0 + 64].rearrange("p (g c) -> p g c", g=2)
        lo_mask, hi_mask, row16 = (cst[:, c:c + 1] for c in (MASK0, MASK0 + 1, MASK0 + 2))
        index = cst[:, INDEX0:INDEX0 + E]
        convw_sb = sb("convw_sb", [128, QK + C])
        convb_sb = sb("convb_sb", [QK, 2])
        bv_sb = sb("bv_sb", [128, C])
        gamma_sb = sb("gamma_sb", [128, 1])
        attw_sb = sb("attw_sb", [128, 5 * 128])
        gate_sb = sb("gate_sb", [128, E])
        b2_sb = sb("b2_sb", [E, 128])
        raw = [sb(f"raw{s}", [128, 2 * HID]) for s in range(2)]
        b1c = [sb(f"b1c{s}", [128, MT]) for s in range(2)]
        wst = [[sb(f"wst{s}_{n}", [128, HID], f32r) for n in ("w1h", "w1l", "w2h", "w2l")] for s in range(2)]

        x_sb = sb("x_sb", [128, T])
        t1 = sb("t1", [128, T])
        t2 = sb("t2", [128, T])
        xn = sb("xn", [128, T])
        dev = sb("dev", [128, T])
        sq = sb("sq", [128, T])
        table = sb("table", [1, 2])

        combB = sb("combB", [128, NHALF, E, HALF])
        room = combB[:, :, :, :].rearrange("p a e t -> p (a e t)")
        A = room[:, 0:2048].rearrange("p (k j v) -> p k j v", k=W, j=J)
        S = room[:, 2048:4096].rearrange("p (q j k v) -> p q j k v", q=KQ, j=J, k=K4)
        AT = room[:, 4096:6144].rearrange("p (t n) -> p t n", t=2)
        vT = room[:, 6144:7168].rearrange("p (i c) -> p i c", c=C)
        x_kh = room[:, 7168:8192]
        cq = xn[0:C8, :]
        ck = dev[0:C8, :]
        nv, ny, na = (sb(n, [128, TILES]) for n in ("nv", "ny", "na"))
        cmax = sb("cmax", [128, KQ, J, K4])
        csum = sb("csum", [128, KQ, K4 * J])
        crcp = sb("crcp", [128, KQ, K4 * J])

        kh = [sb(f"kh{g}", [128, T], f32r) for g in range(2)]
        kl = [sb(f"kl{g}", [128, T], f32r) for g in range(2)]
        qh = [sb(f"qh{g}", [128, HALF], f32r) for g in range(2)]
        qs = [sb(f"qs{g}", [128, T], f32r) for g in range(2)]
        q1 = [sb(f"q1{g}", [128, T], f32r) for g in range(2)]
        vpad = sb("vpad", [128, T // 128, HEADS, 32])
        nmx = sb("nmx", [128, 2, T // 128, 128])
        probs = sb("probs", [128, 2, 4, 2, TOK])
        att = sb("att", [128, 2, TOK])

        g_top = sb("g_top", [128, TILES, 8])
        g_at = sb("g_at", [128, TILES, 8], mybir.dt.uint32)
        g_oh1 = sb("g_oh1", [128, TILES, E])
        g_oh2 = sb("g_oh2", [128, TILES, E])
        g_gap, g_exp, g_sum, g_rcp = (sb(n, [128, TILES]) for n in ("g_gap", "g_exp", "g_sum", "g_rcp"))
        comb = sb("comb", [128, NHALF, TILES, E])
        combT = sb("combT", [E, T])

        x2h = sb("x2h", [128, T], f32r)
        x2l = sb("x2l", [128, T], f32r)
        G = sb("G", [128, GR, HALF])
        hh = [sb(f"hh{i}", [128, HALF], f32r) for i in range(HR)]
        hl = [sb(f"hl{i}", [128, HALF], f32r) for i in range(HR)]
        part = sb("part", [128, 2, HALF])

        PS = ctx.enter_context(nc.psum_tensor("PS", [128, 8, 512], f32))

        x_in_s = [sem(f"x_in{p}") for p in range(NHALF)]
        x_kh_in, bv_in = sem("x_kh_in"), sem("bv_in")
        convw_in, attw_in, cst_in, w_in = sem("convw_in"), sem("attw_in"), sem("cst_in"), [sem(f"w_in{s}") for s in range(2)]
        whi1_ready, whi2_ready = sem("whi1_ready"), sem("whi2_ready")
        b1_in = [sem(f"b1_in{s}") for s in range(2)]
        proj_done, cq_ready, ck_ready = sem("proj_done"), sem("cq_ready"), sem("ck_ready")
        vT_done, vT_ready, energy_done = sem("vT_done"), sem("vT_ready"), sem("energy_done")
        cmax_ready, shifted, exp_ready = sem("cmax_ready"), sem("shifted"), sem("exp_ready")
        csum_ready, crcp_ready, A_ready = sem("csum_ready"), sem("crcp_ready"), sem("A_ready")
        A_out = [sem(f"A_out{i}") for i in range(KQ)]
        AT_in = [sem(f"AT_in{i}") for i in range(KQ)]
        conv_done, t1_ready = sem("conv_done"), sem("t1_ready")
        table_loaded = sem("table_loaded")
        mean_done, dev_ready, sq_ready = sem("mean_done"), sem("dev_ready"), sem("sq_ready")
        var_done, spread_done, rstd_ready, xn_ready = sem("var_done"), sem("spread_done"), sem("rstd_ready"), sem("xn_ready")
        qkv_done, hi_ready, lo_ready = sem("qkv_done"), sem("hi_ready"), sem("lo_ready")
        v_done, v_ready, vzero = sem("v_done"), sem("v_ready"), sem("vzero")
        raw_done, max_ready, q1_ready = sem("raw_done"), sem("max_ready"), sem("q1_ready")
        nmT_done, nmT_ready = sem("nmT_done"), sem("nmT_ready")
        score_done, prob_ready, pv_done = sem("score_done"), sem("prob_ready"), sem("pv_done")
        rcp_ready, att_ready, t2_ready = sem("rcp_ready"), sem("att_ready"), sem("t2_ready")
        logits_done, x2h_ready, x2l_ready = sem("logits_done"), sem("x2h_ready"), sem("x2l_ready")
        gstep, gap_ready, gexp_ready, comb_ready = sem("gstep"), sem("gap_ready"), sem("gexp_ready"), sem("comb_ready")
        onehot_ready, gsum_ready, grcp_ready = sem("onehot_ready"), sem("gsum_ready"), sem("grcp_ready")
        combT_done, combT_ready, bias_done, acc_ready = sem("combT_done"), sem("combT_ready"), sem("bias_done"), sem("acc_ready")
        combB_done, combB_ready = sem("combB_done"), sem("combB_ready")
        wlo1_ready, wlo2_ready, up_done, gelu_done = sem("wlo1_ready"), sem("wlo2_ready"), sem("up_done"), sem("gelu_done")
        hh_ready, hl_ready, down_done = sem("hh_ready"), sem("hl_ready"), sem("down_done")
        part_ready, acc_done, out_sent = sem("part_ready"), sem("acc_done"), sem("out_sent")

        block = ctx.enter_context(nc.Block())

        def cols(p):
            return slice(p * HALF, (p + 1) * HALF)

        RAW_SLOTS = [[(4, 5), (6, 7)], [(5,), (6,), (7,)]]
        SCORE_SLOTS = [[(0, 1), (2, 3)], [(4,), (5,), (6,)]]
        PV_BANK = [6, 7, 7, 7]
        SLOTS = [4 // len(RAW_SLOTS[p][0]) for p in range(NHALF)]

        def slots_before(p, n):
            return 4 * sum(SLOTS[:p]) + n * SLOTS[p]

        VISITS = NHALF * E
        LAG = 3
        FREE = 12
        WEIGH_LAG = 8

        MEAN_BANK = [0, 4, 4, 4]
        VAR_BANK = [1, 5, 5, 5]

        QK_BANK = [0, 1, 2, 3]
        V_BANK = [4, 6]
        U_BANK, Y_BANK, GATE_BANK = (0, 1), (2, 3), 4

        GATING = [0, 31]
        RAW0, RAW_STEPS, SCORES, UNIT_STEPS, ATTEND_LAST, NORM = 1, 12, 14, 3, 24, 28
        G_LOGITS, G_ORDER, G_EXP, G_WEIGHTS, G_ROWS, G_BIAS, G_SPREAD = 0, 1, 3, 3, 5, 6, 7
        LAST_UNIT = 7

        def raw_slots(n):
            n -= RAW0
            if n < 0 or n >= RAW_STEPS:
                return []
            slots = TILES * SLOTS[1]
            return [(TILES + r // SLOTS[1], r % SLOTS[1])
                    for r in range(n * slots // RAW_STEPS, (n + 1) * slots // RAW_STEPS)]

        def scores_unit(n):
            u, rest = divmod(n - SCORES, UNIT_STEPS)
            return 4 + u if rest == 0 and 0 <= u < 4 else None

        def attend_unit(n):
            return LAST_UNIT if n == ATTEND_LAST else scores_unit(n - UNIT_STEPS) if n < ATTEND_LAST else None

        def spread_experts(g):
            return range(E)[2 * (g - G_SPREAD):2 * (g - G_SPREAD + 1)] if g >= G_SPREAD else []

        @block.sync
        def _(sp):
            for p in range(NHALF):
                sp.dma_start(x_sb[:, cols(p)], x_in[:, cols(p)]).then_inc(x_in_s[p], 16)
            sp.dma_start(x_kh[:, :], x_kh_in_dram).then_inc(x_kh_in, 16)
            sp.dma_start(attw_sb[:, :], attw).then_inc(attw_in, 16)
            def visit_weights(k, s):
                e = k % E if isinstance(k, int) else k - E
                if not (isinstance(k, int) and k < 2):
                    sp.wait_ge(wlo2_ready, k - 1)
                sp.dma_start(raw[s][:, :], w12[bass.ds(e, 1), :, :].rearrange("a p n -> (a p) n")).then_inc(w_in[s], 16)
                if not (isinstance(k, int) and k < 2):
                    sp.wait_ge(gelu_done, MT * (k - 1))
                sp.dma_start(b1c[s][:, :], b1[bass.ds(e, 1), :, :].rearrange("a p n -> (a p) n")).then_inc(b1_in[s], 16)

            for k in range(2):
                visit_weights(k, k)
            for q in range(KQ):
                sp.wait_ge(A_ready, q + 1)
                sp.dma_start(scratch[q], A[:, q * K4:(q + 1) * K4, :, :].rearrange("p k j v -> p (k j v)"))\
                    .then_inc(A_out[q], 16)
            for q in range(KQ):
                sp.wait_ge(A_out[q], 16)
                src = scratch[q].rearrange("(bw h) (k r) -> (h k) bw r", h=H, k=K4)
                dst = AT[64 * (q % 2):64 * (q % 2) + 64, q // 2, :].rearrange("p (bw r) -> p bw r", bw=2 * B)
                sp.dma_start(dst, src).then_inc(AT_in[q], 16)
            for k in range(2, FREE):
                visit_weights(k, k % 2)
            with sp.Fori(FREE // 2, VISITS // 2) as i:
                for s in range(2):
                    visit_weights(2 * i + s, s)
            for p in range(NHALF):
                sp.wait_ge(acc_done, E * (p + 1))
                sp.dma_start(out[:, cols(p)], t2[:, cols(p)]).then_inc(out_sent, 16)
            sp.wait_ge(out_sent, 16 * NHALF)

        @block.gpsimd
        def _(pool):
            nc.gpsimd.memset(vpad[:, :, :, :], 0.0).then_inc(vzero, 1)
            nc.gpsimd.memset(nmx[:, :, :, :], 0.0).then_inc(vzero, 1)
            for q in range(KQ):
                pool.wait_ge(crcp_ready, q + 1)
                a = A[:, q * K4:(q + 1) * K4, :, :].rearrange("p k j v -> p (k j) v")
                nc.gpsimd.tensor_tensor(a, a, crcp[:, q, :].unsqueeze(2).broadcast_to([128, K4 * J, W]), ALU.mult)\
                    .then_inc(A_ready, 1)

            def low_weights(k, s, n):
                pool.wait_ge((whi1_ready, whi2_ready)[n], k + 1)
                nc.gpsimd.tensor_tensor(wst[s][2 * n + 1][:, :], raw[s][:, n * HID:(n + 1) * HID],
                                        wst[s][2 * n][:, :].bitcast(f32), ALU.subtract)\
                    .then_inc((wlo1_ready, wlo2_ready)[n], 1)

            def accumulate(k, s, p):
                pool.wait_ge(part_ready, k + 1)
                if isinstance(k, int) and k % E == 0:
                    pool.wait_ge(acc_ready, p + 1)
                if not (isinstance(k, int) and k == 0):
                    pool.wait_ge(acc_done, k)
                nc.gpsimd.tensor_tensor(t2[:, cols(p)], t2[:, cols(p)], part[:, s, :], ALU.add).then_inc(acc_done, 1)

            for k in range(2):
                low_weights(k, k, 0)
                low_weights(k, k, 1)
            for k in range(1, FREE):
                if k > 1:
                    low_weights(k, k % 2, 0)
                    low_weights(k, k % 2, 1)
                if k >= 3:
                    accumulate(k - 3, (k - 3) % 2, (k - 3) // E)
            for k in range(FREE, E + 4):
                low_weights(k, k % 2, 0)
                low_weights(k, k % 2, 1)
                accumulate(k - 3, (k - 3) % 2, (k - 3) // E)
            with pool.Fori((E + 4) // 2, VISITS // 2) as i:
                for s in range(2):
                    low_weights(2 * i + s, s, 0)
                    low_weights(2 * i + s, s, 1)
                    accumulate(2 * i + s - 3, 1 - s, 1)
            for k in range(VISITS - 3, VISITS):
                accumulate(k, k % 2, 1)

        @block.scalar
        def _(act):
            act.dma_start(convw_sb[:, :], convw).then_inc(convw_in, 16)
            act.dma_start(convb_sb[:, :], convb).then_inc(convw_in, 16)
            act.dma_start(bv_sb[:, :], bv.partition_broadcast(128)).then_inc(bv_in, 16)
            act.dma_start(gamma_sb[:, :], gamma.partition_broadcast(128)).then_inc(bv_in, 16)
            act.dma_start(cst[:, :], consts).then_inc(cst_in, 16)
            act.dma_start(gate_sb[:, :], gate).then_inc(cst_in, 16)
            act.dma_start(b2_sb[:, :], b2).then_inc(cst_in, 16)
            act.wait_ge(convw_in, 32)
            for p in range(NHALF):
                act.wait_ge(proj_done, p + 1)
                for b in range(2):
                    nc.scalar.activation(
                        cq[:, (2 * p + b) * TOK:(2 * p + b + 1) * TOK].rearrange("c (j w h) -> c h w j", j=J, w=W2N),
                        PS[0:C8, p, b * TOK:(b + 1) * TOK].rearrange("c (h w j) -> c h w j", h=H, w=W2N),
                        ACT.Identity, bias=convb_sb[0:C8, 0:1]).then_inc(cq_ready, 1)
            for q in range(KQ):
                act.wait_ge(shifted, q + 1)
                nc.scalar.activation(A[:, q * K4:(q + 1) * K4, :, :].rearrange("p k j v -> p j k v"), S[:, q],
                                     ACT.Exp).then_inc(exp_ready, 1)
            act.wait_ge(cst_in, 48)

            def load_table(function):
                nc.scalar.activation(table[0:1, 0:1], cst[0:1, 0:1], function).then_inc(table_loaded, 1)

            def norm_square(n):
                act.wait_ge(dev_ready, n + 1)
                nc.scalar.activation(sq[:, cols(n % 2)], dev[:, cols(n % 2)], ACT.Square).then_inc(sq_ready, 1)

            def high_weights(k, s, n):
                if n == 0:
                    act.wait_ge(w_in[s], 8 * (k - s) + 16)
                if not (isinstance(k, int) and k < 2):
                    act.wait_ge((up_done, down_done)[n], MT * (k - 1))
                nc.scalar.activation(wst[s][2 * n][:, :], raw[s][:, n * HID:(n + 1) * HID], ACT.Copy)\
                    .then_inc((whi1_ready, whi2_ready)[n], 1)

            def high_part(p, n):
                g = n % 2
                act.wait_ge(qkv_done, 4 * p + n + 1)
                if n < 2:
                    nc.scalar.activation(kh[g][:, cols(p)], PS[:, QK_BANK[n], :], ACT.Copy).then_inc(hi_ready, 1)
                else:
                    if p:
                        act.wait_ge(lo_ready, n + 1)
                    nc.scalar.activation(qh[g][:, :], PS[:, QK_BANK[n], :], ACT.Copy).then_inc(hi_ready, 1)
                    nc.scalar.activation(q1[g][:, cols(p)], PS[:, QK_BANK[n], :], ACT.Identity, scale=hi_mask,
                                         bias=row16).then_inc(q1_ready, 1)

            def exps(u, s):
                p = u // 4
                banks = SCORE_SLOTS[p][(SLOTS[p] * (u % 4) + s) % len(SCORE_SLOTS[p])]
                w = len(banks)
                act.wait_ge(score_done, slots_before(p, u % 4) + s + 1)
                if u >= 2:
                    act.wait_ge(pv_done, u - 1)
                nc.scalar.activation(probs[:, u % 2, w * s:w * s + w, :, :].rearrange("p a b c -> p (a b c)"),
                                     PS[:, banks[0]:banks[0] + w, :].rearrange("p a b -> p (a b)"), ACT.Exp,
                                     scale=DK ** -0.5).then_inc(prob_ready, 1)

            def gate_exp(p):
                act.wait_ge(gap_ready, p + 1)
                nc.scalar.activation(g_exp[:, :], g_gap[:, :], ACT.Exp).then_inc(gexp_ready, 1)

            def comb_copy(p, e):
                act.wait_ge(combB_done, p * E + e + 1)
                nc.scalar.activation(combB[:, p, e, :], PS[:, GATE_BANK, :], ACT.Copy).then_inc(combB_ready, 1)

            def gelu(n, k, s):
                if s % MT == 0:
                    act.wait_ge(b1_in[s // MT], 8 * (k - s // MT) + 16)
                act.wait_ge(up_done, n + 1)
                if not (isinstance(n, int) and n < GR):
                    act.wait_ge(hl_ready, n - GR + 1)
                bias = b1c[s // MT][:, s % MT:s % MT + 1]
                nc.scalar.activation(G[:, s % GR, :], PS[:, U_BANK[s % 2], :], ACT.Gelu, bias=bias)\
                    .then_inc(gelu_done, 1)

            for k in range(2):
                high_weights(k, k, 0)
                high_weights(k, k, 1)
            norm_square(0)
            load_table(ACT.Exp)
            for n in range(4):
                high_part(0, n)
            for u in range(4):
                for s in range(SLOTS[0]):
                    exps(u, s)
                if u == 0:
                    norm_square(1)
            norm_square(2)
            high_part(1, 0)
            for n in range(1, 4):
                high_part(1, n)
            load_table(ACT.Gelu)
            for n in range(MT * FREE):
                if scores_unit(n):
                    for s in range(SLOTS[1]):
                        exps(scores_unit(n), s)
                k = n // MT
                gelu(n, k, n % (2 * MT))
                if k and n % MT == 0:
                    high_weights(k + 1, (k + 1) % 2, 0)
                if k and n % MT == MT - 1:
                    high_weights(k + 1, (k + 1) % 2, 1)
                for p in range(NHALF):
                    g = n - GATING[p]
                    if g == G_EXP:
                        gate_exp(p)
                    for e in spread_experts(g):
                        comb_copy(p, e)
                if n == NORM:
                    norm_square(3)

            def gelus(i, last):
                for s in range(2 * MT):
                    k = 2 * i + s // MT
                    gelu(2 * MT * i + s, k, s)
                    if not (last and s >= MT):
                        if s % MT == 0:
                            high_weights(k + 1, 1 - s // MT, 0)
                        if s % MT == MT - 1:
                            high_weights(k + 1, 1 - s // MT, 1)

            with act.Fori(FREE // 2, VISITS // 2 - 1) as i:
                gelus(i, False)
            gelus(VISITS // 2 - 1, True)

        @block.vector
        def _(dve):
            dve.wait_ge(convw_in, 32)
            for p in range(NHALF):
                dve.wait_ge(proj_done, p + 1)
                nc.vector.tensor_scalar(ck[:, cols(p)], PS[32:QK, p, :], convb_sb[32:QK, 1:2], None, ALU.add)\
                    .then_inc(ck_ready, 1)
            dve.wait_ge(bv_in, 32)
            for i in range(2):
                dve.wait_ge(vT_done, i + 1)
                nc.vector.tensor_tensor(vT[:, 4 * i:4 * i + 4, :],
                                        PS[:, 4 + i, :].rearrange("p (a c) -> p a c", c=C),
                                        bv_sb[:, :].unsqueeze(1).broadcast_to([128, 4, C]), ALU.add).then_inc(vT_ready, 1)

            def shift(q):
                e = PS[:, q, :].rearrange("p (j k v) -> p j k v", j=J, k=K4)
                dve.wait_ge(energy_done, q + 1)
                nc.vector.tensor_reduce(cmax[:, q], e, AX.X, ALU.max).then_inc(cmax_ready, 1)
                dve.wait_ge(cmax_ready, q + 1)
                nc.vector.tensor_tensor(S[:, q], e, cmax[:, q].unsqueeze(3).broadcast_to([128, J, K4, W]),
                                        ALU.subtract).then_inc(shifted, 1)

            def sums(q):
                dve.wait_ge(exp_ready, q + 1)
                nc.vector.tensor_reduce(csum[:, q], A[:, q * K4:(q + 1) * K4, :, :].rearrange("p k j v -> p (k j) v"),
                                        AX.X, ALU.add).then_inc(csum_ready, 1)
                dve.wait_ge(csum_ready, q + 1)
                nc.vector.reciprocal(crcp[:, q], csum[:, q]).then_inc(crcp_ready, 1)

            shift(0)
            for q in range(1, KQ):
                shift(q)
                sums(q - 1)
            sums(KQ - 1)
            dve.wait_ge(cst_in, 48)
            def conv_add(p):
                dve.wait_ge(conv_done, 2 * (p + 1))
                if p == 0:
                    for q in range(NHALF):
                        dve.wait_ge(x_in_s[q], 16)
                nc.vector.scalar_tensor_tensor(
                    t1[:, cols(p)].rearrange("p (b n) -> p b n", b=2), PS[:, 4 + 2 * p:6 + 2 * p, 0:TOK],
                    gamma_sb[:, 0:1], x_sb[:, cols(p)].rearrange("p (b n) -> p b n", b=2),
                    ALU.mult, ALU.add).then_inc(t1_ready, 1)

            steps = [0]

            def then(ins):
                steps[0] += 1
                ins.then_inc(gstep, 1)
                dve.wait_ge(gstep, steps[0])

            def norm_dev(n):
                src = (t1, t2)[n // 2]
                dve.wait_ge(mean_done, n + 1)
                nc.vector.tensor_tensor(dev[:, cols(n % 2)], src[:, cols(n % 2)], PS[:, MEAN_BANK[n], :],
                                        ALU.subtract).then_inc(dev_ready, 1)

            def norm_rstd(n):
                dve.wait_ge(var_done, n + 1)
                then(nc.vector.tensor_scalar(nv[:, :], PS[:, VAR_BANK[n], 0:TILES], 0.5, 0.5 * EPS, ALU.mult, ALU.add))
                then(nc.vector.tensor_scalar(ny[:, :].bitcast(i32), nv[:, :].bitcast(i32), -0.5, RSQRT_MAGIC,
                                             ALU.mult, ALU.add))
                for k in range(3):
                    then(nc.vector.tensor_tensor(na[:, :], ny[:, :], ny[:, :], ALU.mult))
                    then(nc.vector.scalar_tensor_tensor(na[:, :], na[:, :], -1.0, nv[:, :], ALU.mult, ALU.mult))
                    last = nc.vector.scalar_tensor_tensor(ny[:, :], na[:, :], 1.5, ny[:, :], ALU.add, ALU.mult)
                    if k < 2:
                        then(last)
                last.then_inc(rstd_ready, 1)

            def norm_out(n):
                dve.wait_ge(spread_done, n + 1)
                nc.vector.tensor_tensor(xn[:, cols(n % 2)], dev[:, cols(n % 2)], PS[:, VAR_BANK[n], :],
                                        ALU.mult).then_inc(xn_ready, 1)

            def low_part(p, n):
                g = n % 2
                dve.wait_ge(hi_ready, 4 * p + n + 1)
                if n < 2:
                    nc.vector.tensor_tensor(kl[g][:, cols(p)], PS[:, QK_BANK[n], :], kh[g][:, cols(p)].bitcast(f32),
                                            ALU.subtract).then_inc(lo_ready, 1)
                else:
                    dve.wait_ge(q1_ready, 2 * p + g + 1)
                    nc.vector.scalar_tensor_tensor(qs[g][:, cols(p)], qh[g][:, :].bitcast(f32), lo_mask,
                                                   PS[:, QK_BANK[n], :], ALU.mult, ALU.add).then_inc(lo_ready, 1)

            def values(p):
                dve.wait_ge(v_done, p + 1)
                dst = vpad[:, TILES * p:TILES * (p + 1), :, :].rearrange("p t h c -> p (t h c)")\
                    .rearrange("p (th r) -> p th r", r=64)
                src = PS[:, V_BANK[p], :].rearrange("p (th r) -> p th r", r=32)
                for par in range(2):
                    nc.vector.tensor_copy(dst[:, :, 48 * par:48 * par + DK], src[:, :, DK * par:DK * (par + 1)])\
                        .then_inc(v_ready, 1)

            def raw_max(t, s):
                p = t // TILES
                n = slots_before(p, t % TILES) + s
                banks = RAW_SLOTS[p][(n - slots_before(p, 0)) % len(RAW_SLOTS[p])]
                w = len(banks)
                dve.wait_ge(raw_done, n + 1)
                cols16 = nmx[:, :, t, :].rearrange("p g (j c) -> p j g c", c=32)[:, w * s:w * s + w, :, DK]
                nc.vector.tensor_reduce(cols16, PS[:, banks[0]:banks[0] + w, :].rearrange("p b (g m) -> p b g m", g=2),
                                        AX.X, ALU.max, negate=True).then_inc(max_ready, 1)

            def max_rows(p):
                for g in range(2):
                    dve.wait_ge(nmT_done, 2 * p + g + 1)
                    nc.vector.tensor_tensor(kl[g][:, cols(p)], kl[g][:, cols(p)].bitcast(f32), PS[:, 4 + g, :],
                                            ALU.add).then_inc(nmT_ready, 1)

            def attend(b):
                tok = slice(b * TOK, (b + 1) * TOK)
                dve.wait_ge(pv_done, 2 * (b + 1))
                nc.vector.reciprocal(att[:, b % 2, :], PS[:, PV_BANK[b], TOK:2 * TOK]).then_inc(rcp_ready, 1)
                dve.wait_ge(rcp_ready, b + 1)
                nc.vector.tensor_tensor(att[:, b % 2, :], PS[:, PV_BANK[b], 0:TOK], att[:, b % 2, :], ALU.mult)                    .then_inc(att_ready, 1)
                dve.wait_ge(att_ready, b + 1)
                nc.vector.tensor_tensor(t2[:, tok], t1[:, tok], att[:, b % 2, :], ALU.add).then_inc(t2_ready, 1)

            def split_x2(p):
                dve.wait_ge(xn_ready, NHALF + p + 1)
                nc.vector.tensor_copy(x2h[:, cols(p)], xn[:, cols(p)]).then_inc(x2h_ready, 1)
                dve.wait_ge(x2h_ready, p + 1)
                nc.vector.tensor_tensor(x2l[:, cols(p)], xn[:, cols(p)], x2h[:, cols(p)].bitcast(f32), ALU.subtract)\
                    .then_inc(x2l_ready, 1)

            def spread(v):
                return v.unsqueeze(2).broadcast_to([128, TILES, E])

            def top_logits(p):
                dve.wait_ge(logits_done, p + 1)
                for t in range(TILES):
                    last = nc.vector.max(g_top[:, t, :], PS[:, GATE_BANK, t * E:(t + 1) * E])
                then(last)

            def top_experts(p):
                for t in range(TILES):
                    last = nc.vector.max_index(g_at[:, t, :], g_top[:, t, :], PS[:, GATE_BANK, t * E:(t + 1) * E])
                then(last)
                nc.vector.tensor_tensor(g_gap[:, :], g_top[:, :, 1], g_top[:, :, 0], ALU.subtract)\
                    .then_inc(gap_ready, 1)
                for k, onehot in enumerate((g_oh1, g_oh2)):
                    nc.vector.tensor_tensor(onehot[:, :, :], index.unsqueeze(1).broadcast_to([128, TILES, E]),
                                            spread(g_at[:, :, k]), ALU.is_equal).then_inc(onehot_ready, 1)

            def top_weights(p):
                dve.wait_ge(gexp_ready, p + 1)
                dve.wait_ge(onehot_ready, 2 * (p + 1))
                nc.vector.tensor_scalar(g_sum[:, :], g_exp[:, :], 1.0, None, ALU.add).then_inc(gsum_ready, 1)
                then(nc.vector.tensor_tensor(g_oh2[:, :, :], g_oh2[:, :, :], spread(g_exp[:, :]), ALU.mult))
                dve.wait_ge(gsum_ready, p + 1)
                nc.vector.reciprocal(g_rcp[:, :], g_sum[:, :]).then_inc(grcp_ready, 1)
                then(nc.vector.tensor_tensor(g_oh1[:, :, :], g_oh1[:, :, :], g_oh2[:, :, :], ALU.add))
                dve.wait_ge(grcp_ready, p + 1)
                nc.vector.tensor_tensor(comb[:, p], g_oh1[:, :, :], spread(g_rcp[:, :]), ALU.mult)\
                    .then_inc(comb_ready, 1)

            def comb_rows(p):
                dve.wait_ge(combT_done, p + 1)
                nc.vector.tensor_copy(combT[:, cols(p)], PS[0:E, GATE_BANK, :]).then_inc(combT_ready, 1)

            def bias_sum(p):
                dve.wait_ge(bias_done, p + 1)
                nc.vector.tensor_tensor(t2[:, cols(p)], t2[:, cols(p)], PS[:, GATE_BANK, :], ALU.add).then_inc(acc_ready, 1)

            def parts(n, s):
                dve.wait_ge(gelu_done, n + 1)
                if not (isinstance(n, int) and n < HR):
                    dve.wait_ge(down_done, n - HR + 1)
                nc.vector.tensor_copy(hh[s % HR][:, :], G[:, s % GR, :]).then_inc(hh_ready, 1)
                dve.wait_ge(hh_ready, n + 1)
                nc.vector.tensor_tensor(hl[s % HR][:, :], G[:, s % GR, :], hh[s % HR][:, :].bitcast(f32), ALU.subtract)\
                    .then_inc(hl_ready, 1)

            def weigh(k, s):
                dve.wait_ge(down_done, MT * (k + 1))
                if isinstance(k, int):
                    if k < 2:
                        dve.wait_ge(combB_ready, k + 1)
                    else:
                        dve.wait_ge(acc_done, k - 1)
                        dve.wait_ge(combB_ready, k + 1)
                    weights = combB[:, k // E, k % E, :]
                else:
                    dve.wait_ge(acc_done, k - 1)
                    weights = combB[:, 1, bass.ds(k - E, 1), :].rearrange("p a t -> p (a t)")
                nc.vector.tensor_tensor(part[:, s, :], PS[:, Y_BANK[s], :], weights, ALU.mult).then_inc(part_ready, 1)

            conv_add(0)
            norm_dev(0)
            conv_add(1)
            norm_rstd(0)
            norm_out(0)
            for n in range(4):
                low_part(0, n)
            dve.wait_ge(vzero, 2)
            values(0)
            for t in range(TILES):
                for s in range(SLOTS[0]):
                    raw_max(t, s)
            max_rows(0)
            norm_dev(1)
            norm_rstd(1)
            norm_out(1)
            attend(0)
            attend(1)
            norm_dev(2)
            low_part(1, 0)
            norm_rstd(2)
            norm_out(2)
            split_x2(0)
            for n in range(1, 4):
                low_part(1, n)
            values(1)
            for n in range(MT * FREE):
                for t, s in raw_slots(n):
                    raw_max(t, s)
                parts(n, n % (2 * MT))
                if n >= WEIGH_LAG and n % MT == 0:
                    k = (n - WEIGH_LAG) // MT
                    weigh(k, k % 2)
                for p in range(NHALF):
                    g = n - GATING[p]
                    if g == G_LOGITS:
                        top_logits(p)
                    if g == G_ORDER:
                        top_experts(p)
                    if g == G_WEIGHTS:
                        top_weights(p)
                    if g == G_ROWS:
                        comb_rows(p)
                    if g == G_BIAS:
                        bias_sum(p)
                if n == RAW0 + RAW_STEPS:
                    max_rows(1)
                if attend_unit(n - 1) in (5, 7):
                    attend(attend_unit(n - 1) // 2)
                if n == NORM:
                    norm_dev(3)
                if n == NORM + 1:
                    norm_rstd(3)
                if n == NORM + 2:
                    norm_out(3)
                    split_x2(1)
            with dve.Fori(FREE // 2, VISITS // 2) as i:
                for s in range(2 * MT):
                    parts(2 * MT * i + s, s)
                    if s % MT == 0:
                        weigh(2 * i + s // MT - WEIGH_LAG // MT, s // MT)
            for k in range(VISITS - WEIGH_LAG // MT, VISITS):
                weigh(k, k % 2)

        @block.tensor
        def _(pe):
            mm = nc.tensor.matmul
            pe.wait_ge(convw_in, 32)
            for p in range(NHALF):
                pe.wait_ge(x_in_s[p], 16)
                mm(PS[0:QK, p, :], convw_sb[:, 0:QK], x_sb[:, cols(p)], start=True, stop=True).then_inc(proj_done, 1)
            pe.wait_ge(x_kh_in, 16)
            for b in range(B):
                for kt in range(2):
                    i = 2 * b + kt
                    toks = x_kh[:, i * 128:(i + 1) * 128]
                    last = mm(PS[:, 4 + i // 4, (i % 4) * C:(i % 4 + 1) * C], toks, convw_sb[:, QK:QK + C],
                              start=True, stop=True)
                if b % 2:
                    last.then_inc(vT_done, 1)
            pe.wait_ge(cq_ready, B)
            pe.wait_ge(ck_ready, NHALF)
            for q in range(KQ):
                for j in range(J):
                    for b in range(B):
                        rows = cq[:, b * TOK + j * 32:b * TOK + (j + 1) * 32]
                        last = mm(PS[32 * b:32 * (b + 1), q, j * K4 * W:(j + 1) * K4 * W], rows,
                                  ck[:, b * TOK + q * K4 * W:b * TOK + (q + 1) * K4 * W], start=True, stop=True)
                last.then_inc(energy_done, 1)
            pe.wait_ge(vT_ready, 2)
            def conv_apply(b, kt):
                last = mm(PS[:, 4 + b, 0:TOK], vT[:, 2 * b + kt, :], AT[:, kt, b * TOK:(b + 1) * TOK],
                          start=(kt == 0), stop=(kt == 1))
                if kt:
                    last.then_inc(conv_done, 1)

            def norm_mean(n):
                p = n % 2
                pe.wait_ge((t1_ready, t2_ready)[n // 2], 2 * (p + 1) if n // 2 else p + 1)
                if n == 1:
                    pe.wait_ge(nmT_ready, 2)
                mm(PS[:, MEAN_BANK[n], :], avg, (t1, t2)[n // 2][:, cols(p)], start=True, stop=True)\
                    .then_inc(mean_done, 1)

            def norm_var(n):
                pe.wait_ge(sq_ready, n + 1)
                for t in range(TILES):
                    last = mm(PS[:, VAR_BANK[n], t:t + 1],
                              sq[:, n % 2 * HALF + t * 128:n % 2 * HALF + (t + 1) * 128], avg[:, 0:1],
                              start=True, stop=True)
                last.then_inc(var_done, 1)

            def norm_spread(n):
                pe.wait_ge(rstd_ready, n + 1)
                for t in range(TILES):
                    last = nc.tensor.transpose(PS[:, VAR_BANK[n], t * 128:(t + 1) * 128],
                                               ny[:, t:t + 1].broadcast_to([128, 128]), ident)
                last.then_inc(spread_done, 1)

            def project(p, n):
                if n == 0:
                    pe.wait_ge(xn_ready, p + 1)
                mm(PS[:, QK_BANK[n], :], attw_sb[:, n * 128:(n + 1) * 128], xn[:, cols(p)], start=True, stop=True)\
                    .then_inc(qkv_done, 1)

            def project_v(p):
                for t in range(TILES):
                    last = mm(PS[:, V_BANK[p], t * 128:(t + 1) * 128],
                              xn[:, p * HALF + t * 128:p * HALF + (t + 1) * 128],
                              attw_sb[:, 512:640], start=True, stop=True)
                last.then_inc(v_done, 1)

            def head_rows(j):
                return slice(32 * j, 32 * j + 32)

            def raw_scores(t, s):
                p, b = t // TILES, t // 2
                n = slots_before(p, t % TILES) + s
                if s == 0 and t % TILES == 0:
                    pe.wait_ge(lo_ready, 4 * (p + 1))
                    pe.wait_ge(v_ready, 2 * (p + 1))
                if n == 1:
                    pe.wait_ge(t1_ready, 2)
                slots = RAW_SLOTS[p]
                at = n - slots_before(p, 0)
                if at >= len(slots):
                    pe.wait_ge(max_ready, n - len(slots) + 1)
                banks = slots[at % len(slots)]
                for a, bank in enumerate(banks):
                    j = len(banks) * s + a
                    for g in range(2):
                        last = mm(PS[:, bank, g * TOK:(g + 1) * TOK], kh[g][head_rows(j), t * 128:(t + 1) * 128],
                                  qs[g][head_rows(j), b * TOK:(b + 1) * TOK], start=True, stop=True)
                last.then_inc(raw_done, 1)

            def max_transpose(p):
                pe.wait_ge(max_ready, slots_before(p, 4))
                if p:
                    pe.wait_ge(combB_ready, E)
                for g in range(2):
                    for t in range(TILES):
                        last = nc.tensor.transpose(PS[:, 4 + g, t * 128:(t + 1) * 128], nmx[:, g, TILES * p + t, :],
                                                   ident)
                    last.then_inc(nmT_done, 1)

            def scores(u, s):
                b, g, p = u // 2, u % 2, u // 4
                pe.wait_ge(nmT_ready, 4 if p else g + 1)
                n = slots_before(p, u % 4) + s
                if n - len(SCORE_SLOTS[p]) >= slots_before(p, 0):
                    pe.wait_ge(prob_ready, n - len(SCORE_SLOTS[p]) + 1)
                tok = slice(b * TOK, (b + 1) * TOK)
                slots = SCORE_SLOTS[p]
                banks = slots[(SLOTS[p] * (u % 4) + s) % len(slots)]
                for a, bank in enumerate(banks):
                    rows = head_rows(len(banks) * s + a)
                    for mt in range(2):
                        o = PS[:, bank, mt * TOK:(mt + 1) * TOK]
                        m = slice(b * TOK + mt * 128, b * TOK + (mt + 1) * 128)
                        mm(o, qs[g][rows, m], kh[g][rows, tok], start=True, stop=False)
                        last = mm(o, q1[g][rows, m], kl[g][rows, tok], start=False, stop=True)
                last.then_inc(score_done, 1)

            def attend(u, sums):
                b, g, p = u // 2, u % 2, u // 4
                if not sums:
                    pe.wait_ge(prob_ready, slots_before(p, u % 4 + 1))
                    if g == 0 and b >= 1 and PV_BANK[b] == PV_BANK[b - 1]:
                        pe.wait_ge(t2_ready, b)
                for mt in range(2):
                    for j in range(4):
                        wt = ones_par[:, g, :] if sums else vpad[:, 2 * b + mt, 2 * j + g, :]
                        last = mm(PS[head_rows(j), PV_BANK[b], sums * TOK:(sums + 1) * TOK], wt,
                                  probs[:, u % 2, j, mt, :], start=(not sums and g == 0 and mt == 0),
                                  stop=(g == 1 and mt == 1), skip_group_check=True)
                if sums:
                    last.then_inc(pv_done, 1)

            def logits(p):
                pe.wait_ge(xn_ready, NHALF + p + 1)
                for t in range(TILES):
                    last = mm(PS[:, GATE_BANK, t * E:(t + 1) * E], xn[:, p * HALF + t * 128:p * HALF + (t + 1) * 128],
                              gate_sb[:, :], start=True, stop=True)
                last.then_inc(logits_done, 1)

            def comb_rows(p):
                pe.wait_ge(comb_ready, p + 1)
                for t in range(TILES):
                    last = nc.tensor.transpose(PS[0:E, GATE_BANK, t * 128:(t + 1) * 128], comb[:, p, t, :], ident)
                last.then_inc(combT_done, 1)

            def bias_product(p):
                pe.wait_ge(combT_ready, p + 1)
                mm(PS[:, GATE_BANK, :], b2_sb[:, :], combT[:, cols(p)], start=True, stop=True).then_inc(bias_done, 1)

            def comb_spread(p, e):
                pe.wait_ge(*((combB_ready, p * E + e) if e else (acc_ready, p + 1)))
                for t in range(TILES):
                    last = nc.tensor.transpose(PS[:, GATE_BANK, t * 128:(t + 1) * 128],
                                               comb[:, p, t, e:e + 1].broadcast_to([128, 128]), ident)
                last.then_inc(combB_done, 1)

            def up(n, k, s):
                w, m = wst[s // MT], s % MT
                p = k // E if isinstance(k, int) else 1
                if m == 0:
                    pe.wait_ge(wlo1_ready, k + 1)
                if not (isinstance(n, int) and n < 2):
                    pe.wait_ge(gelu_done, n - 1)
                if isinstance(n, int) and n % (MT * E) == 0:
                    pe.wait_ge(x2l_ready, p + 1)
                if isinstance(n, int) and n == 0:
                    pe.wait_ge(lo_ready, 8)
                o, ms = PS[:, U_BANK[s % 2], :], slice(m * 128, (m + 1) * 128)
                mm(o, w[0][:, ms], x2h[:, cols(p)], start=True, stop=False)
                mm(o, w[0][:, ms], x2l[:, cols(p)], start=False, stop=False)
                mm(o, w[1][:, ms], x2h[:, cols(p)], start=False, stop=True).then_inc(up_done, 1)

            def down(n, k, s):
                w, m = wst[s // MT], s % MT
                if m == 0:
                    pe.wait_ge(wlo2_ready, k + 1)
                    if not (isinstance(k, int) and k < 2):
                        pe.wait_ge(part_ready, k - 1)
                pe.wait_ge(hl_ready, n + 1)
                o, ms = PS[:, Y_BANK[s // MT], :], slice(m * 128, (m + 1) * 128)
                mm(o, w[2][:, ms], hh[s % HR][:, :], start=(m == 0), stop=False)
                mm(o, w[3][:, ms], hh[s % HR][:, :], start=False, stop=False)
                mm(o, w[2][:, ms], hl[s % HR][:, :], start=False, stop=(m == MT - 1)).then_inc(down_done, 1)

            pe.wait_ge(cst_in, 48)
            for kt in range(2):
                pe.wait_ge(AT_in[2 * kt], 16)
                pe.wait_ge(AT_in[2 * kt + 1], 16)
                for b in range(2):
                    conv_apply(b, kt)
            for kt in range(2):
                conv_apply(2, kt)
            norm_mean(0)
            for kt in range(2):
                conv_apply(3, kt)
            norm_var(0)
            norm_spread(0)
            pe.wait_ge(attw_in, 16)
            for n in range(4):
                project(0, n)
            project_v(0)
            for t in range(TILES):
                for s in range(SLOTS[0]):
                    raw_scores(t, s)
            max_transpose(0)
            for s in range(SLOTS[0]):
                scores(0, s)
            for u in range(4):
                if u == 0:
                    norm_mean(1)
                if u == 1:
                    norm_var(1)
                if u == 2:
                    norm_spread(1)
                if u < 3:
                    for s in range(SLOTS[0]):
                        scores(u + 1, s)
                attend(u, 0)
                attend(u, 1)
            norm_mean(2)
            project(1, 0)
            norm_var(2)
            project(1, 1)
            project(1, 2)
            norm_spread(2)
            project(1, 3)
            project_v(1)

            for n in range(MT * FREE):
                for t, s in raw_slots(n):
                    raw_scores(t, s)
                if scores_unit(n):
                    for s in range(3):
                        scores(scores_unit(n), s)
                up(n, n // MT, n % (2 * MT))
                if scores_unit(n):
                    scores(scores_unit(n), 3)
                for p in range(NHALF):
                    g = n - GATING[p]
                    if g == G_LOGITS:
                        logits(p)
                    if g == G_ROWS:
                        comb_rows(p)
                    if g == G_BIAS:
                        bias_product(p)
                    for e in spread_experts(g)[:1]:
                        comb_spread(p, e)
                if n == RAW0 + RAW_STEPS:
                    max_transpose(1)
                if n == NORM:
                    norm_mean(3)
                if n == NORM + 1:
                    norm_var(3)
                if n >= LAG:
                    down(n - LAG, (n - LAG) // MT, (n - LAG) % (2 * MT))
                for p in range(NHALF):
                    for e in spread_experts(n - GATING[p])[1:]:
                        comb_spread(p, e)
                if attend_unit(n):
                    attend(attend_unit(n), 0)
                    attend(attend_unit(n), 1)
                if n == NORM + 2:
                    norm_spread(3)
            with pe.Fori(FREE // 2, VISITS // 2) as i:
                for s in range(2 * MT):
                    up(2 * MT * i + s, 2 * i + s // MT, s)
                    back = (s - LAG) % (2 * MT)
                    down(2 * MT * i + s - LAG, 2 * i + (s - LAG) // MT, back)
            for n in range(MT * VISITS - LAG, MT * VISITS):
                down(n, n // MT, n % (2 * MT))


def kernel(**inputs):
    import concourse.bacc as bacc
    from concourse.bass_utils import run_bass_kernel_spmd

    a = {k: np.asarray(v) for k, v in inputs.items()}

    def by_parity(w):
        w = w.reshape(C, HEADS // 2, 2, 1, DK).transpose(0, 2, 1, 3, 4)
        return np.broadcast_to(w, (C, 2, HEADS // 2, 2, DK)).reshape(C, 256)

    consts = np.zeros((128, CONSTS), np.float32)
    consts[:, ID0:ID0 + 128] = np.eye(128)
    consts[:, AVG0:AVG0 + 128] = 1.0 / C
    consts[:, ONE0:ONE0 + DK] = 1.0
    consts[:, ONE0 + 32 + DK:ONE0 + 64] = 1.0
    consts[:, MASK0] = np.where(np.arange(128) % 32 < DK, 0.0, -1.0)
    consts[:, MASK0 + 1] = np.arange(128) % 32 < DK
    consts[:, MASK0 + 2] = np.arange(128) % 32 == DK
    consts[:, INDEX0:INDEX0 + E] = np.arange(E)

    arrays = {
        "x": a["x"].reshape(B, C, TOK).transpose(1, 0, 2).reshape(C, T),
        "x_kh": a["x"].reshape(B, C, H, KQ, K4).transpose(1, 0, 3, 2, 4).reshape(C, T),
        "convw": np.concatenate([a["L0_conv_wq"].T, np.zeros((C, 32 - C8), np.float32), a["L0_conv_wk"].T,
                                 a["L0_conv_wv"].T], axis=1),
        "convb": np.stack([np.pad(a["L0_conv_bq"], (0, 32)), np.pad(a["L0_conv_bk"], (32, 0))], axis=1),
        "bv": a["L0_conv_bv"],
        "gamma": a["L0_conv_gamma"],
        "attw": np.concatenate([by_parity(a["L1_attn_Wk"]), by_parity(a["L1_attn_Wq"]), a["L1_attn_Wv"]], axis=1),
        "gate": a["L1_ffn_gate_w"].T,
        "w12": np.concatenate([a["L1_ffn_w1"].transpose(0, 2, 1),
                               a["L1_ffn_w2"].reshape(E, C, MT, 128).transpose(0, 3, 2, 1).reshape(E, 128, HID)],
                              axis=2),
        "b1": a["L1_ffn_b1"].reshape(E, MT, 128).transpose(0, 2, 1),
        "b2": a["L1_ffn_b2"],
        "consts": consts,
    }
    arrays = {k: np.ascontiguousarray(v) for k, v in arrays.items()}
    nc = bacc.Bacc("TRN2", target_bir_lowering=False, num_devices=1)
    args = [nc.dram_tensor(k, v.shape, mybir.dt.from_np(v.dtype), kind="ExternalInput").ap()
            for k, v in arrays.items()]
    out = nc.dram_tensor("out", (C, T), mybir.dt.float32, kind="ExternalOutput").ap()
    hybrid_program(nc, *args, out)
    r = run_bass_kernel_spmd(nc, [arrays], core_ids=[0])
    return r.results[0]["out"].reshape(C, B, H, W).transpose(1, 0, 2, 3)
```

```python
import numpy as np

import concourse.bass as bass
from concourse import mybir
from concourse.alu_op_type import AluOpType as ALU
from contextlib import ExitStack

B, C, H, W = 4, 128, 16, 16
TOK = H * W
T = B * TOK
HALF = T // 2
NHALF = T // HALF
C8 = C // 8
QK = 32 + C8
HEADS, DK = 8, 16
E, HID = 8, 512
MT = HID // 128
W2N = 2
J = W // W2N
KQ, K4 = 4, 4
TILES = HALF // 128
EPS = 1e-5
GR, HR = 4, 4
BIG = 1e38
RSQRT_MAGIC = float(0x5F3759DF - (1 << 22))

ID0, AVG0, ONE0, MASK0, INDEX0, CONSTS = 0, 128, 256, 320, 323, 331


def hybrid_program(nc, x_in, x_kh_in_dram, convw, convb, bv, gamma, attw, gate, w12, b1, b2, consts, out):
    f32, f32r, i32 = mybir.dt.float32, mybir.dt.float32r, mybir.dt.int32
    ACT = mybir.ActivationFunctionType
    AX = mybir.AxisListType
    scratch = nc.dram_tensor("attn_scratch", (KQ, 128, K4 * J * W), f32, kind="Internal").ap()
    comb_rows_dram = nc.dram_tensor("comb_rows", (NHALF, E, HALF), f32, kind="Internal").ap()

    with ExitStack() as ctx:
        def sb(name, shape, dt=f32):
            return ctx.enter_context(nc.sbuf_tensor(name, shape, dt))

        def sem(name):
            return ctx.enter_context(nc.semaphore(name))

        cst = sb("cst", [128, CONSTS])
        ident, avg = cst[:, ID0:ID0 + 128], cst[:, AVG0:AVG0 + 128]
        ones_par = cst[:, ONE0:ONE0 + 64].rearrange("p (g c) -> p g c", g=2)
        lo_mask, hi_mask, row16 = (cst[:, c:c + 1] for c in (MASK0, MASK0 + 1, MASK0 + 2))
        index = cst[:, INDEX0:INDEX0 + E]
        convw_sb = sb("convw_sb", [128, QK + C])
        convb_sb = sb("convb_sb", [QK, 2])
        bv_sb = sb("bv_sb", [128, C])
        gamma_sb = sb("gamma_sb", [128, 1])
        attw_sb = sb("attw_sb", [128, 5 * 128])
        gate_sb = sb("gate_sb", [128, E])
        b2_sb = sb("b2_sb", [128, E])
        raw = [sb(f"raw{s}", [128, 2 * HID]) for s in range(2)]
        b1_sb = sb("b1_sb", [128, E * MT])
        b1c = [sb(f"b1c{s}", [128, MT]) for s in range(2)]
        wst = [[sb(f"wst{s}_{n}", [128, HID], f32r) for n in ("w1h", "w1l", "w2h", "w2l")] for s in range(2)]

        x_sb = sb("x_sb", [128, T])
        t1 = sb("t1", [128, T])
        t2 = sb("t2", [128, T])
        xn = sb("xn", [128, T])
        dev = sb("dev", [128, T])
        sq = sb("sq", [128, T])
        table = sb("table", [1, 1])

        combB = sb("combB", [128, NHALF, E, HALF])
        room = combB[:, :, :, :].rearrange("p a e t -> p (a e t)")
        A = room[:, 0:2048].rearrange("p (k j v) -> p k j v", k=W, j=J)
        S = room[:, 2048:4096].rearrange("p (q j k v) -> p q j k v", q=KQ, j=J, k=K4)
        AT = room[:, 4096:6144].rearrange("p (t n) -> p t n", t=2)
        vT = room[:, 6144:7168].rearrange("p (i c) -> p i c", c=C)
        x_kh = room[:, 7168:8192]
        cq = xn[0:C8, :]
        ck = dev[0:C8, :]
        nv, ny, na = (sb(n, [128, TILES]) for n in ("nv", "ny", "na"))
        cmax = sb("cmax", [128, KQ, J, K4])
        csum = sb("csum", [128, KQ, K4 * J])
        crcp = sb("crcp", [128, KQ, K4 * J])

        kh = [sb(f"kh{g}", [128, T], f32r) for g in range(2)]
        kl = [sb(f"kl{g}", [128, T], f32r) for g in range(2)]
        qh = [sb(f"qh{g}", [128, HALF], f32r) for g in range(2)]
        qs = [sb(f"qs{g}", [128, T], f32r) for g in range(2)]
        q1 = [sb(f"q1{g}", [128, T], f32r) for g in range(2)]
        vpad = sb("vpad", [128, T // 128, HEADS, 32])
        nmx = sb("nmx", [128, 2, T // 128, 128])
        probs = sb("probs", [128, 2, 4, 2, TOK])
        pairs = sb("pairs", [128, 2, 4, TOK])
        att = sb("att", [128, 2, TOK])

        g_top = sb("g_top", [128, TILES, 8])
        g_at = sb("g_at", [128, TILES, 8], mybir.dt.uint32)
        g_oh1 = sb("g_oh1", [128, TILES, E])
        g_oh2 = sb("g_oh2", [128, TILES, E])
        g_gap, g_exp, g_sum, g_rcp = (sb(n, [128, TILES]) for n in ("g_gap", "g_exp", "g_sum", "g_rcp"))
        comb = sb("comb", [128, NHALF, TILES, E])
        combT = sb("combT", [E, T])

        x2h = sb("x2h", [128, T], f32r)
        x2l = sb("x2l", [128, T], f32r)
        G = sb("G", [128, GR, HALF])
        hh = [sb(f"hh{i}", [128, HALF], f32r) for i in range(HR)]
        hl = [sb(f"hl{i}", [128, HALF], f32r) for i in range(HR)]
        part = sb("part", [128, 2, HALF])

        PS = ctx.enter_context(nc.psum_tensor("PS", [128, 8, 512], f32))

        x_in_s = [sem(f"x_in{p}") for p in range(NHALF)]
        x_kh_in, bv_in = sem("x_kh_in"), sem("bv_in")
        convw_in, attw_in, cst_in, w_in = sem("convw_in"), sem("attw_in"), sem("cst_in"), [sem(f"w_in{s}") for s in range(2)]
        whi1_ready, whi2_ready = sem("whi1_ready"), sem("whi2_ready")
        b1_in = [sem(f"b1_in{s}") for s in range(2)]
        proj_done, cq_ready, ck_ready = sem("proj_done"), sem("cq_ready"), sem("ck_ready")
        vT_done, vT_ready, energy_done = sem("vT_done"), sem("vT_ready"), sem("energy_done")
        cmax_ready, shifted, exp_ready = sem("cmax_ready"), sem("shifted"), sem("exp_ready")
        csum_ready, crcp_ready, A_ready = sem("csum_ready"), sem("crcp_ready"), sem("A_ready")
        A_out = [sem(f"A_out{i}") for i in range(KQ)]
        AT_in = [sem(f"AT_in{i}") for i in range(KQ)]
        conv_done, t1_ready = sem("conv_done"), sem("t1_ready")
        table_loaded = sem("table_loaded")
        mean_done, dev_ready, sq_ready = sem("mean_done"), sem("dev_ready"), sem("sq_ready")
        var_done, spread_done, rstd_ready, xn_ready = sem("var_done"), sem("spread_done"), sem("rstd_ready"), sem("xn_ready")
        qkv_done, hi_ready, lo_ready = sem("qkv_done"), sem("hi_ready"), sem("lo_ready")
        v_done, v_ready, vzero = sem("v_done"), sem("v_ready"), sem("vzero")
        raw_done, max_ready, q1_ready = sem("raw_done"), sem("max_ready"), sem("q1_ready")
        nmT_done, nmT_ready = sem("nmT_done"), sem("nmT_ready")
        score_done, prob_ready, paired, pv_done = sem("score_done"), sem("prob_ready"), sem("paired"), sem("pv_done")
        rcp_ready, att_ready, t2_ready = sem("rcp_ready"), sem("att_ready"), sem("t2_ready")
        logits_done, x2h_ready, x2l_ready = sem("logits_done"), sem("x2h_ready"), sem("x2l_ready")
        gstep, gap_ready, gexp_ready, comb_ready = sem("gstep"), sem("gap_ready"), sem("gexp_ready"), sem("comb_ready")
        onehot_ready, gsum_ready, grcp_ready = sem("onehot_ready"), sem("gsum_ready"), sem("grcp_ready")
        combT_done, combT_ready, comb_out = sem("combT_done"), sem("combT_ready"), sem("comb_out")
        combB_in = [sem(f"combB_in{e}") for e in range(E)]
        wlo1_ready, wlo2_ready, up_done, gelu_done = sem("wlo1_ready"), sem("wlo2_ready"), sem("up_done"), sem("gelu_done")
        hh_ready, hl_ready, down_done = sem("hh_ready"), sem("hl_ready"), sem("down_done")
        part_ready, acc_done, out_sent = sem("part_ready"), sem("acc_done"), sem("out_sent")

        block = ctx.enter_context(nc.Block())

        def cols(p):
            return slice(p * HALF, (p + 1) * HALF)

        RAW_SLOTS = [[(4, 5), (6, 7)], [(5,), (6,), (7,)]]
        SCORE_SLOTS = [[(0, 1), (2, 3)], [(4,), (5,), (6,)]]
        PV_BANK = [6, 7, 7, 7]
        SLOTS = [4 // len(RAW_SLOTS[p][0]) for p in range(NHALF)]

        def slots_before(p, n):
            return 4 * sum(SLOTS[:p]) + n * SLOTS[p]

        VISITS = NHALF * E
        LAG = 3
        FREE = 12
        WEIGH_LAG = 8
        GATING_LAG = [0, 1]

        MEAN_BANK = [0, 4, 4, 4]
        VAR_BANK = [1, 5, 5, 5]

        QK_BANK = [0, 1, 2, 3]
        V_BANK = [4, 6]
        U_BANK, Y_BANK, GATE_BANK = (0, 1), (2, 3), 4

        GATING = [0, 32]
        RAW0, RAW_STEPS, SCORES, UNIT_STEPS, ATTEND_LAST, NORM = 1, 12, 14, 3, 24, 26
        G_LOGITS, G_ORDER, G_EXP, G_WEIGHTS, G_ROWS = 0, 1, 2, 2, 4
        HH_BY_ACT = 14
        COMB_AFTER = [3, 11]
        LAST_UNIT = 2 * B - 1

        def raw_slots(n):
            n -= RAW0
            if n < 0 or n >= RAW_STEPS:
                return []
            slots = TILES * SLOTS[1]
            return [(TILES + r // SLOTS[1], r % SLOTS[1])
                    for r in range(n * slots // RAW_STEPS, (n + 1) * slots // RAW_STEPS)]

        def scores_unit(n):
            u, rest = divmod(n - SCORES, UNIT_STEPS)
            return 4 + u if rest == 0 and 0 <= u < 4 else None

        def attend_unit(n):
            return LAST_UNIT if n == ATTEND_LAST else scores_unit(n - UNIT_STEPS) if n < ATTEND_LAST else None

        def weigh_visit(n):
            for k in range(VISITS):
                if n == MT * k + WEIGH_LAG + (GATING_LAG[k // E] if k % E == 0 else 0):
                    return k
            return None

        @block.sync
        def _(sp):
            for p in range(NHALF):
                sp.dma_start(x_sb[:, cols(p)], x_in[:, cols(p)]).then_inc(x_in_s[p], 16)
            sp.dma_start(x_kh[:, :], x_kh_in_dram).then_inc(x_kh_in, 16)
            sp.dma_start(attw_sb[:, :], attw).then_inc(attw_in, 16)

            def visit_weights(k, s):
                e = k % E if isinstance(k, int) else k - E
                if not (isinstance(k, int) and k < 2):
                    sp.wait_ge(wlo2_ready, k - 1)
                sp.dma_start(raw[s][:, :], w12[bass.ds(e, 1), :, :].rearrange("a p n -> (a p) n")).then_inc(w_in[s], 16)

            def visit_bias(k, s):
                if not (isinstance(k, int) and k < FREE + 2):
                    sp.wait_ge(gelu_done, MT * (k - 1))
                e = k - E
                sp.dma_start(b1c[s][:, :], b1[:, bass.ds(MT * e, MT)]).then_inc(b1_in[s], 16)

            for k in range(2):
                visit_weights(k, k)
            for q in range(KQ):
                sp.wait_ge(A_ready, q + 1)
                sp.dma_start(scratch[q], A[:, q * K4:(q + 1) * K4, :, :].rearrange("p k j v -> p (k j v)"))\
                    .then_inc(A_out[q], 16)
            for q in range(KQ):
                sp.wait_ge(A_out[q], 16)
                src = scratch[q].rearrange("(bw h) (k r) -> (h k) bw r", h=H, k=K4)
                dst = AT[64 * (q % 2):64 * (q % 2) + 64, q // 2, :].rearrange("p (bw r) -> p bw r", bw=2 * B)
                sp.dma_start(dst, src).then_inc(AT_in[q], 16)

            def comb_everywhere(p, part):
                if part == 0:
                    sp.wait_ge(combT_ready, p + 1)
                    sp.dma_start(comb_rows_dram[p], combT[:, cols(p)]).then_inc(comb_out, 16)
                    sp.wait_ge(comb_out, 16 * (p + 1))
                for e in range(E)[part * E // 2:(part + 1) * E // 2]:
                    sp.dma_start(combB[:, p, e, :], comb_rows_dram[p, e, :].partition_broadcast(128))\
                        .then_inc(combB_in[e], 16)

            for k in range(FREE, FREE + 2):
                visit_bias(k, k % 2)
            for k in range(2, FREE + 2):
                visit_weights(k, k % 2)
                for part in range(2):
                    if k - part in COMB_AFTER:
                        comb_everywhere(COMB_AFTER.index(k - part), part)
            with sp.Fori(FREE // 2 + 1, VISITS // 2) as i:
                for s in range(2):
                    visit_weights(2 * i + s, s)
                    visit_bias(2 * i + s, s)
            for p in range(NHALF):
                sp.wait_ge(acc_done, E * (p + 1))
                sp.dma_start(out[:, cols(p)], t2[:, cols(p)]).then_inc(out_sent, 16)
            sp.wait_ge(out_sent, 16 * NHALF)

        @block.gpsimd
        def _(pool):
            nc.gpsimd.memset(vpad[:, :, :, :], 0.0).then_inc(vzero, 1)
            nc.gpsimd.memset(nmx[:, :, :, :], 0.0).then_inc(vzero, 1)
            for q in range(KQ):
                pool.wait_ge(crcp_ready, q + 1)
                a = A[:, q * K4:(q + 1) * K4, :, :].rearrange("p k j v -> p (k j) v")
                nc.gpsimd.tensor_tensor(a, a, crcp[:, q, :].unsqueeze(2).broadcast_to([128, K4 * J, W]), ALU.mult)\
                    .then_inc(A_ready, 1)

            def low_weights(k, s, n):
                pool.wait_ge((whi1_ready, whi2_ready)[n], k + 1)
                nc.gpsimd.tensor_tensor(wst[s][2 * n + 1][:, :], raw[s][:, n * HID:(n + 1) * HID],
                                        wst[s][2 * n][:, :].bitcast(f32), ALU.subtract)\
                    .then_inc((wlo1_ready, wlo2_ready)[n], 1)

            def pair(u, s):
                p = u // 4
                w = len(SCORE_SLOTS[p][0])
                pool.wait_ge(prob_ready, slots_before(p, u % 4) + s + 1)
                if u >= 2:
                    pool.wait_ge(pv_done, u - 1)
                a = probs[:, u % 2, w * s:w * s + w, :, :]
                nc.gpsimd.tensor_tensor(pairs[:, u % 2, w * s:w * s + w, :], a[:, :, 0, :], a[:, :, 1, :], ALU.add)\
                    .then_inc(paired, 1)

            def accumulate(k, s, p):
                pool.wait_ge(part_ready, k + 1)
                if not (isinstance(k, int) and k == 0):
                    pool.wait_ge(acc_done, k)
                nc.gpsimd.tensor_tensor(t2[:, cols(p)], t2[:, cols(p)], part[:, s, :], ALU.add).then_inc(acc_done, 1)

            for k in range(2):
                low_weights(k, k, 0)
                low_weights(k, k, 1)
            for u in range(4):
                for s in range(SLOTS[0]):
                    pair(u, s)
            for n in range(MT * FREE - MT):
                if scores_unit(n):
                    for s in range(SLOTS[1]):
                        pair(scores_unit(n), s)
                k = n // MT
                if k and n % MT == 0:
                    low_weights(k + 1, (k + 1) % 2, 0)
                if k and n % MT == MT - 1:
                    low_weights(k + 1, (k + 1) % 2, 1)
                if n >= WEIGH_LAG and n % MT == 0:
                    k = (n - WEIGH_LAG) // MT
                    accumulate(k, k % 2, k // E)
            with pool.Fori(FREE // 2, VISITS // 2) as i:
                for s in range(2):
                    low_weights(2 * i + s, s, 0)
                    low_weights(2 * i + s, s, 1)
                    accumulate(2 * i + s - 3, 1 - s, 1)
            for k in range(VISITS - 3, VISITS):
                accumulate(k, k % 2, 1)

        @block.scalar
        def _(act):
            act.dma_start(convw_sb[:, :], convw).then_inc(convw_in, 16)
            act.dma_start(convb_sb[:, :], convb).then_inc(convw_in, 16)
            act.dma_start(bv_sb[:, :], bv.partition_broadcast(128)).then_inc(bv_in, 16)
            act.dma_start(gamma_sb[:, :], gamma.partition_broadcast(128)).then_inc(bv_in, 16)
            act.dma_start(cst[:, :], consts).then_inc(cst_in, 16)
            act.dma_start(gate_sb[:, :], gate).then_inc(cst_in, 16)
            act.dma_start(b2_sb[:, :], b2).then_inc(cst_in, 16)
            act.dma_start(b1_sb[:, :], b1).then_inc(cst_in, 16)
            act.wait_ge(convw_in, 32)
            for p in range(NHALF):
                act.wait_ge(proj_done, p + 1)
                for b in range(2):
                    nc.scalar.activation(
                        cq[:, (2 * p + b) * TOK:(2 * p + b + 1) * TOK].rearrange("c (j w h) -> c h w j", j=J, w=W2N),
                        PS[0:C8, p, b * TOK:(b + 1) * TOK].rearrange("c (h w j) -> c h w j", h=H, w=W2N),
                        ACT.Identity, bias=convb_sb[0:C8, 0:1]).then_inc(cq_ready, 1)
            for q in range(KQ):
                act.wait_ge(shifted, q + 1)
                nc.scalar.activation(A[:, q * K4:(q + 1) * K4, :, :].rearrange("p k j v -> p j k v"), S[:, q],
                                     ACT.Exp).then_inc(exp_ready, 1)
            act.wait_ge(cst_in, 64)

            def load_table(function):
                nc.scalar.activation(table[0:1, 0:1], cst[0:1, 0:1], function).then_inc(table_loaded, 1)

            def norm_square(n):
                act.wait_ge(dev_ready, n + 1)
                nc.scalar.activation(sq[:, cols(n % 2)], dev[:, cols(n % 2)], ACT.Square).then_inc(sq_ready, 1)

            def high_weights(k, s, n):
                if n == 0:
                    act.wait_ge(w_in[s], 8 * (k - s) + 16)
                if not (isinstance(k, int) and k < 2):
                    act.wait_ge((up_done, down_done)[n], MT * (k - 1))
                nc.scalar.activation(wst[s][2 * n][:, :], raw[s][:, n * HID:(n + 1) * HID], ACT.Copy)\
                    .then_inc((whi1_ready, whi2_ready)[n], 1)

            def high_part(p, n):
                g = n % 2
                act.wait_ge(qkv_done, 4 * p + n + 1)
                if n < 2:
                    nc.scalar.activation(kh[g][:, cols(p)], PS[:, QK_BANK[n], :], ACT.Copy).then_inc(hi_ready, 1)
                else:
                    if p:
                        act.wait_ge(lo_ready, n + 1)
                    nc.scalar.activation(qh[g][:, :], PS[:, QK_BANK[n], :], ACT.Copy).then_inc(hi_ready, 1)
                    nc.scalar.activation(q1[g][:, cols(p)], PS[:, QK_BANK[n], :], ACT.Identity, scale=hi_mask,
                                         bias=row16).then_inc(q1_ready, 1)

            def exps(u, s):
                p = u // 4
                banks = SCORE_SLOTS[p][(SLOTS[p] * (u % 4) + s) % len(SCORE_SLOTS[p])]
                w = len(banks)
                act.wait_ge(score_done, slots_before(p, u % 4) + s + 1)
                if u >= 2:
                    act.wait_ge(pv_done, u - 1)
                nc.scalar.activation(probs[:, u % 2, w * s:w * s + w, :, :].rearrange("p a b c -> p (a b c)"),
                                     PS[:, banks[0]:banks[0] + w, :].rearrange("p a b -> p (a b)"), ACT.Exp,
                                     scale=DK ** -0.5).then_inc(prob_ready, 1)

            def gate_exp(p):
                act.wait_ge(gap_ready, p + 1)
                nc.scalar.activation(g_exp[:, :], g_gap[:, :], ACT.Exp).then_inc(gexp_ready, 1)

            def gelu(n, k, s):
                if isinstance(k, int) and k < FREE:
                    bias = b1_sb[:, MT * (k % E) + s % MT:MT * (k % E) + s % MT + 1]
                else:
                    bias = b1c[s // MT][:, s % MT:s % MT + 1]
                    if s % MT == 0:
                        act.wait_ge(b1_in[s // MT], 8 * (k - FREE - s // MT) + 16)
                act.wait_ge(up_done, n + 1)
                if not (isinstance(n, int) and n < GR):
                    act.wait_ge(hl_ready, n - GR + 1)
                if isinstance(n, int) and n < HH_BY_ACT:
                    if n >= HR:
                        act.wait_ge(down_done, n - HR + 1)
                    nc.scalar.activation(hh[s % HR][:, :], PS[:, U_BANK[s % 2], :], ACT.Gelu, bias=bias)\
                        .then_inc(hh_ready, 1)
                nc.scalar.activation(G[:, s % GR, :], PS[:, U_BANK[s % 2], :], ACT.Gelu, bias=bias)\
                    .then_inc(gelu_done, 1)

            for k in range(2):
                high_weights(k, k, 0)
                high_weights(k, k, 1)
            norm_square(0)
            load_table(ACT.Exp)
            for n in range(4):
                high_part(0, n)
            for u in range(4):
                for s in range(SLOTS[0]):
                    exps(u, s)
                if u == 0:
                    norm_square(1)
            high_part(1, 0)
            norm_square(2)
            for n in range(1, 4):
                high_part(1, n)
            load_table(ACT.Gelu)
            for n in range(MT * FREE):
                if scores_unit(n):
                    for s in range(SLOTS[1]):
                        exps(scores_unit(n), s)
                k = n // MT
                gelu(n, k, n % (2 * MT))
                if n == NORM:
                    norm_square(3)
                if k and n % MT == 0:
                    high_weights(k + 1, (k + 1) % 2, 0)
                if k and n % MT == MT - 1:
                    high_weights(k + 1, (k + 1) % 2, 1)
                for p in range(NHALF):
                    g = n - GATING[p]
                    if g == G_EXP:
                        gate_exp(p)

            def gelus(i, last):
                for s in range(2 * MT):
                    k = 2 * i + s // MT
                    gelu(2 * MT * i + s, k, s)
                    if not (last and s >= MT):
                        if s % MT == 0:
                            high_weights(k + 1, 1 - s // MT, 0)
                        if s % MT == MT - 1:
                            high_weights(k + 1, 1 - s // MT, 1)

            with act.Fori(FREE // 2, VISITS // 2 - 1) as i:
                gelus(i, False)
            gelus(VISITS // 2 - 1, True)

        @block.vector
        def _(dve):
            dve.wait_ge(convw_in, 32)
            for p in range(NHALF):
                dve.wait_ge(proj_done, p + 1)
                nc.vector.tensor_scalar(ck[:, cols(p)], PS[32:QK, p, :], convb_sb[32:QK, 1:2], None, ALU.add)\
                    .then_inc(ck_ready, 1)
            dve.wait_ge(bv_in, 32)
            for i in range(2):
                dve.wait_ge(vT_done, i + 1)
                nc.vector.tensor_tensor(vT[:, 4 * i:4 * i + 4, :],
                                        PS[:, 4 + i, :].rearrange("p (a c) -> p a c", c=C),
                                        bv_sb[:, :].unsqueeze(1).broadcast_to([128, 4, C]), ALU.add).then_inc(vT_ready, 1)

            def shift(q):
                e = PS[:, q, :].rearrange("p (j k v) -> p j k v", j=J, k=K4)
                dve.wait_ge(energy_done, q + 1)
                nc.vector.tensor_reduce(cmax[:, q], e, AX.X, ALU.max).then_inc(cmax_ready, 1)
                dve.wait_ge(cmax_ready, q + 1)
                nc.vector.tensor_tensor(S[:, q], e, cmax[:, q].unsqueeze(3).broadcast_to([128, J, K4, W]),
                                        ALU.subtract).then_inc(shifted, 1)

            def sums(q):
                dve.wait_ge(exp_ready, q + 1)
                nc.vector.tensor_reduce(csum[:, q], A[:, q * K4:(q + 1) * K4, :, :].rearrange("p k j v -> p (k j) v"),
                                        AX.X, ALU.add).then_inc(csum_ready, 1)
                dve.wait_ge(csum_ready, q + 1)
                nc.vector.reciprocal(crcp[:, q], csum[:, q]).then_inc(crcp_ready, 1)

            shift(0)
            for q in range(1, KQ):
                shift(q)
                sums(q - 1)
            sums(KQ - 1)
            dve.wait_ge(cst_in, 64)
            def conv_add(p):
                dve.wait_ge(conv_done, 2 * (p + 1))
                if p == 0:
                    for q in range(NHALF):
                        dve.wait_ge(x_in_s[q], 16)
                nc.vector.scalar_tensor_tensor(
                    t1[:, cols(p)].rearrange("p (b n) -> p b n", b=2), PS[:, 4 + 2 * p:6 + 2 * p, 0:TOK],
                    gamma_sb[:, 0:1], x_sb[:, cols(p)].rearrange("p (b n) -> p b n", b=2),
                    ALU.mult, ALU.add).then_inc(t1_ready, 1)

            steps = [0]

            def then(ins):
                steps[0] += 1
                ins.then_inc(gstep, 1)
                dve.wait_ge(gstep, steps[0])

            def norm_dev(n):
                src = (t1, t2)[n // 2]
                dve.wait_ge(mean_done, n + 1)
                nc.vector.tensor_tensor(dev[:, cols(n % 2)], src[:, cols(n % 2)], PS[:, MEAN_BANK[n], :],
                                        ALU.subtract).then_inc(dev_ready, 1)

            def norm_rstd(n):
                dve.wait_ge(var_done, n + 1)
                then(nc.vector.tensor_scalar(nv[:, :], PS[:, VAR_BANK[n], 0:TILES], 0.5, 0.5 * EPS, ALU.mult, ALU.add))
                then(nc.vector.tensor_scalar(ny[:, :].bitcast(i32), nv[:, :].bitcast(i32), -0.5, RSQRT_MAGIC,
                                             ALU.mult, ALU.add))
                for k in range(3):
                    then(nc.vector.tensor_tensor(na[:, :], ny[:, :], ny[:, :], ALU.mult))
                    then(nc.vector.scalar_tensor_tensor(na[:, :], na[:, :], -1.0, nv[:, :], ALU.mult, ALU.mult))
                    last = nc.vector.scalar_tensor_tensor(ny[:, :], na[:, :], 1.5, ny[:, :], ALU.add, ALU.mult)
                    if k < 2:
                        then(last)
                last.then_inc(rstd_ready, 1)

            def norm_out(n):
                dve.wait_ge(spread_done, n + 1)
                nc.vector.tensor_tensor(xn[:, cols(n % 2)], dev[:, cols(n % 2)], PS[:, VAR_BANK[n], :],
                                        ALU.mult).then_inc(xn_ready, 1)

            def low_part(p, n):
                g = n % 2
                dve.wait_ge(hi_ready, 4 * p + n + 1)
                if n < 2:
                    nc.vector.tensor_tensor(kl[g][:, cols(p)], PS[:, QK_BANK[n], :], kh[g][:, cols(p)].bitcast(f32),
                                            ALU.subtract).then_inc(lo_ready, 1)
                else:
                    dve.wait_ge(q1_ready, 2 * p + g + 1)
                    nc.vector.scalar_tensor_tensor(qs[g][:, cols(p)], qh[g][:, :].bitcast(f32), lo_mask,
                                                   PS[:, QK_BANK[n], :], ALU.mult, ALU.add).then_inc(lo_ready, 1)

            def values(p):
                dve.wait_ge(v_done, p + 1)
                dst = vpad[:, TILES * p:TILES * (p + 1), :, :].rearrange("p t h c -> p (t h c)")\
                    .rearrange("p (th r) -> p th r", r=64)
                src = PS[:, V_BANK[p], :].rearrange("p (th r) -> p th r", r=32)
                for par in range(2):
                    nc.vector.tensor_copy(dst[:, :, 48 * par:48 * par + DK], src[:, :, DK * par:DK * (par + 1)])\
                        .then_inc(v_ready, 1)

            def raw_max(t, s):
                p = t // TILES
                n = slots_before(p, t % TILES) + s
                banks = RAW_SLOTS[p][(n - slots_before(p, 0)) % len(RAW_SLOTS[p])]
                w = len(banks)
                dve.wait_ge(raw_done, n + 1)
                cols16 = nmx[:, :, t, :].rearrange("p g (j c) -> p j g c", c=32)[:, w * s:w * s + w, :, DK]
                nc.vector.tensor_reduce(cols16, PS[:, banks[0]:banks[0] + w, :].rearrange("p b (g m) -> p b g m", g=2),
                                        AX.X, ALU.max, negate=True).then_inc(max_ready, 1)

            def max_rows(p):
                for g in range(2):
                    dve.wait_ge(nmT_done, 2 * p + g + 1)
                    nc.vector.tensor_tensor(kl[g][:, cols(p)], kl[g][:, cols(p)].bitcast(f32), PS[:, 4 + g, :],
                                            ALU.add).then_inc(nmT_ready, 1)

            def attend(b):
                tok = slice(b * TOK, (b + 1) * TOK)
                dve.wait_ge(pv_done, 2 * (b + 1))
                nc.vector.reciprocal(att[:, b % 2, :], PS[:, PV_BANK[b], TOK:2 * TOK]).then_inc(rcp_ready, 1)
                dve.wait_ge(rcp_ready, b + 1)
                nc.vector.tensor_tensor(att[:, b % 2, :], PS[:, PV_BANK[b], 0:TOK], att[:, b % 2, :], ALU.mult)\
                    .then_inc(att_ready, 1)
                dve.wait_ge(att_ready, b + 1)
                nc.vector.tensor_tensor(t2[:, tok], t1[:, tok], att[:, b % 2, :], ALU.add).then_inc(t2_ready, 1)

            def split_x2(p):
                dve.wait_ge(xn_ready, NHALF + p + 1)
                nc.vector.tensor_copy(x2h[:, cols(p)], xn[:, cols(p)]).then_inc(x2h_ready, 1)
                dve.wait_ge(x2h_ready, p + 1)
                nc.vector.tensor_tensor(x2l[:, cols(p)], xn[:, cols(p)], x2h[:, cols(p)].bitcast(f32), ALU.subtract)\
                    .then_inc(x2l_ready, 1)

            def spread(v):
                return v.unsqueeze(2).broadcast_to([128, TILES, E])

            def top_logits(p):
                dve.wait_ge(logits_done, p + 1)
                for t in range(TILES):
                    last = nc.vector.max(g_top[:, t, :], PS[:, GATE_BANK, t * E:(t + 1) * E])
                then(last)

            def top_experts(p):
                for t in range(TILES):
                    last = nc.vector.max_index(g_at[:, t, :], g_top[:, t, :], PS[:, GATE_BANK, t * E:(t + 1) * E])
                then(last)
                nc.vector.tensor_tensor(g_gap[:, :], g_top[:, :, 1], g_top[:, :, 0], ALU.subtract)\
                    .then_inc(gap_ready, 1)
                for k, onehot in enumerate((g_oh1, g_oh2)):
                    nc.vector.tensor_tensor(onehot[:, :, :], index.unsqueeze(1).broadcast_to([128, TILES, E]),
                                            spread(g_at[:, :, k]), ALU.is_equal).then_inc(onehot_ready, 1)

            def top_weights(p):
                dve.wait_ge(gexp_ready, p + 1)
                dve.wait_ge(onehot_ready, 2 * (p + 1))
                nc.vector.tensor_scalar(g_sum[:, :], g_exp[:, :], 1.0, None, ALU.add).then_inc(gsum_ready, 1)
                then(nc.vector.tensor_tensor(g_oh2[:, :, :], g_oh2[:, :, :], spread(g_exp[:, :]), ALU.mult))
                dve.wait_ge(gsum_ready, p + 1)
                nc.vector.reciprocal(g_rcp[:, :], g_sum[:, :]).then_inc(grcp_ready, 1)
                then(nc.vector.tensor_tensor(g_oh1[:, :, :], g_oh1[:, :, :], g_oh2[:, :, :], ALU.add))
                dve.wait_ge(grcp_ready, p + 1)
                nc.vector.tensor_tensor(comb[:, p], g_oh1[:, :, :], spread(g_rcp[:, :]), ALU.mult)\
                    .then_inc(comb_ready, 1)

            def comb_rows(p):
                dve.wait_ge(combT_done, p + 1)
                nc.vector.tensor_copy(combT[:, cols(p)], PS[0:E, GATE_BANK, :]).then_inc(combT_ready, 1)

            def parts(n, s):
                dve.wait_ge(gelu_done, n + 1)
                if not (isinstance(n, int) and n < HR):
                    dve.wait_ge(down_done, n - HR + 1)
                if not (isinstance(n, int) and n < HH_BY_ACT):
                    nc.vector.tensor_copy(hh[s % HR][:, :], G[:, s % GR, :]).then_inc(hh_ready, 1)
                dve.wait_ge(hh_ready, n + 1)
                nc.vector.tensor_tensor(hl[s % HR][:, :], G[:, s % GR, :], hh[s % HR][:, :].bitcast(f32), ALU.subtract)\
                    .then_inc(hl_ready, 1)

            def weigh(k, s):
                dve.wait_ge(down_done, MT * (k + 1))
                if isinstance(k, int):
                    dve.wait_ge(combB_in[k % E], 16 * (k // E + 1))
                    if k >= 2:
                        dve.wait_ge(acc_done, k - 1)
                    bias, weights = b2_sb[:, k % E:k % E + 1], combB[:, k // E, k % E, :]
                else:
                    dve.wait_ge(acc_done, k - 1)
                    bias = b2_sb[:, bass.ds(k - E, 1)]
                    weights = combB[:, 1, bass.ds(k - E, 1), :].rearrange("p a t -> p (a t)")
                nc.vector.scalar_tensor_tensor(part[:, s, :], PS[:, Y_BANK[s], :], bias, weights, ALU.add, ALU.mult)\
                    .then_inc(part_ready, 1)

            conv_add(0)
            norm_dev(0)
            conv_add(1)
            norm_rstd(0)
            norm_out(0)
            for n in range(4):
                low_part(0, n)
            dve.wait_ge(vzero, 2)
            values(0)
            for t in range(TILES):
                for s in range(SLOTS[0]):
                    raw_max(t, s)
            max_rows(0)
            norm_dev(1)
            norm_rstd(1)
            norm_out(1)
            attend(0)
            attend(1)
            low_part(1, 0)
            norm_dev(2)
            norm_rstd(2)
            norm_out(2)
            split_x2(0)
            for n in range(1, 4):
                low_part(1, n)
            values(1)
            for n in range(MT * FREE):
                for t, s in raw_slots(n):
                    raw_max(t, s)
                if n == RAW0 + RAW_STEPS:
                    max_rows(1)
                if attend_unit(n - 1) in (5, 7):
                    attend(attend_unit(n - 1) // 2)
                if n == NORM:
                    norm_dev(3)
                if n == NORM + 2:
                    norm_rstd(3)
                if n == NORM + 3:
                    norm_out(3)
                    split_x2(1)
                k = weigh_visit(n)
                if k is not None:
                    weigh(k, k % 2)
                parts(n, n % (2 * MT))
                for p in range(NHALF):
                    g = n - GATING[p]
                    if g == G_LOGITS:
                        top_logits(p)
                    if g == G_ORDER:
                        top_experts(p)
                    if g == G_WEIGHTS:
                        top_weights(p)
                    if g == G_ROWS:
                        comb_rows(p)
            for e in range(FREE - E - WEIGH_LAG // MT, E):
                dve.wait_ge(combB_in[e], 16 * NHALF)
            with dve.Fori(FREE // 2, VISITS // 2) as i:
                for s in range(2 * MT):
                    parts(2 * MT * i + s, s)
                    if s % MT == 0:
                        weigh(2 * i + s // MT - WEIGH_LAG // MT, s // MT)
            for k in range(VISITS - WEIGH_LAG // MT, VISITS):
                weigh(k, k % 2)

        @block.tensor
        def _(pe):
            mm = nc.tensor.matmul
            pe.wait_ge(convw_in, 32)
            for p in range(NHALF):
                pe.wait_ge(x_in_s[p], 16)
                mm(PS[0:QK, p, :], convw_sb[:, 0:QK], x_sb[:, cols(p)], start=True, stop=True).then_inc(proj_done, 1)
            pe.wait_ge(x_kh_in, 16)
            for b in range(B):
                for kt in range(2):
                    i = 2 * b + kt
                    toks = x_kh[:, i * 128:(i + 1) * 128]
                    last = mm(PS[:, 4 + i // 4, (i % 4) * C:(i % 4 + 1) * C], toks, convw_sb[:, QK:QK + C],
                              start=True, stop=True)
                if b % 2:
                    last.then_inc(vT_done, 1)
            pe.wait_ge(cq_ready, B)
            pe.wait_ge(ck_ready, NHALF)
            for q in range(KQ):
                for j in range(J):
                    for b in range(B):
                        rows = cq[:, b * TOK + j * 32:b * TOK + (j + 1) * 32]
                        last = mm(PS[32 * b:32 * (b + 1), q, j * K4 * W:(j + 1) * K4 * W], rows,
                                  ck[:, b * TOK + q * K4 * W:b * TOK + (q + 1) * K4 * W], start=True, stop=True)
                last.then_inc(energy_done, 1)
            pe.wait_ge(vT_ready, 2)
            def conv_apply(b, kt):
                last = mm(PS[:, 4 + b, 0:TOK], vT[:, 2 * b + kt, :], AT[:, kt, b * TOK:(b + 1) * TOK],
                          start=(kt == 0), stop=(kt == 1))
                if kt:
                    last.then_inc(conv_done, 1)

            def norm_mean(n):
                p = n % 2
                pe.wait_ge((t1_ready, t2_ready)[n // 2], 2 * (p + 1) if n // 2 else p + 1)
                if n == 1:
                    pe.wait_ge(nmT_ready, 2)
                mm(PS[:, MEAN_BANK[n], :], avg, (t1, t2)[n // 2][:, cols(p)], start=True, stop=True)\
                    .then_inc(mean_done, 1)

            def norm_var(n):
                pe.wait_ge(sq_ready, n + 1)
                for t in range(TILES):
                    last = mm(PS[:, VAR_BANK[n], t:t + 1],
                              sq[:, n % 2 * HALF + t * 128:n % 2 * HALF + (t + 1) * 128], avg[:, 0:1],
                              start=True, stop=True)
                last.then_inc(var_done, 1)

            def norm_spread(n):
                pe.wait_ge(rstd_ready, n + 1)
                for t in range(TILES):
                    last = nc.tensor.transpose(PS[:, VAR_BANK[n], t * 128:(t + 1) * 128],
                                               ny[:, t:t + 1].broadcast_to([128, 128]), ident)
                last.then_inc(spread_done, 1)

            def project(p, n):
                if n == 0:
                    pe.wait_ge(xn_ready, p + 1)
                mm(PS[:, QK_BANK[n], :], attw_sb[:, n * 128:(n + 1) * 128], xn[:, cols(p)], start=True, stop=True)\
                    .then_inc(qkv_done, 1)

            def project_v(p):
                for t in range(TILES):
                    last = mm(PS[:, V_BANK[p], t * 128:(t + 1) * 128],
                              xn[:, p * HALF + t * 128:p * HALF + (t + 1) * 128],
                              attw_sb[:, 512:640], start=True, stop=True)
                last.then_inc(v_done, 1)

            def head_rows(j):
                return slice(32 * j, 32 * j + 32)

            def raw_scores(t, s):
                p, b = t // TILES, t // 2
                n = slots_before(p, t % TILES) + s
                if s == 0 and t % TILES == 0:
                    pe.wait_ge(lo_ready, 4 * (p + 1))
                    pe.wait_ge(v_ready, 2 * (p + 1))
                if n == 1:
                    pe.wait_ge(t1_ready, 2)
                slots = RAW_SLOTS[p]
                at = n - slots_before(p, 0)
                if at >= len(slots):
                    pe.wait_ge(max_ready, n - len(slots) + 1)
                banks = slots[at % len(slots)]
                for a, bank in enumerate(banks):
                    j = len(banks) * s + a
                    for g in range(2):
                        last = mm(PS[:, bank, g * TOK:(g + 1) * TOK], kh[g][head_rows(j), t * 128:(t + 1) * 128],
                                  qs[g][head_rows(j), b * TOK:(b + 1) * TOK], start=True, stop=True)
                last.then_inc(raw_done, 1)

            def max_transpose(p):
                pe.wait_ge(max_ready, slots_before(p, 4))
                if p:
                    pe.wait_ge(combT_ready, 1)
                for g in range(2):
                    for t in range(TILES):
                        last = nc.tensor.transpose(PS[:, 4 + g, t * 128:(t + 1) * 128], nmx[:, g, TILES * p + t, :],
                                                   ident)
                    last.then_inc(nmT_done, 1)

            def scores(u, s):
                b, g, p = u // 2, u % 2, u // 4
                pe.wait_ge(nmT_ready, 4 if p else g + 1)
                n = slots_before(p, u % 4) + s
                if n - len(SCORE_SLOTS[p]) >= slots_before(p, 0):
                    pe.wait_ge(prob_ready, n - len(SCORE_SLOTS[p]) + 1)
                tok = slice(b * TOK, (b + 1) * TOK)
                slots = SCORE_SLOTS[p]
                banks = slots[(SLOTS[p] * (u % 4) + s) % len(slots)]
                for a, bank in enumerate(banks):
                    rows = head_rows(len(banks) * s + a)
                    for mt in range(2):
                        o = PS[:, bank, mt * TOK:(mt + 1) * TOK]
                        m = slice(b * TOK + mt * 128, b * TOK + (mt + 1) * 128)
                        mm(o, qs[g][rows, m], kh[g][rows, tok], start=True, stop=False)
                        last = mm(o, q1[g][rows, m], kl[g][rows, tok], start=False, stop=True)
                last.then_inc(score_done, 1)

            def attend(u, sums):
                b, g, p = u // 2, u % 2, u // 4
                if not sums:
                    pe.wait_ge(prob_ready, slots_before(p, u % 4 + 1))
                    if g == 0 and b >= 1 and PV_BANK[b] == PV_BANK[b - 1]:
                        pe.wait_ge(t2_ready, b)
                    for mt in range(2):
                        for j in range(4):
                            mm(PS[head_rows(j), PV_BANK[b], 0:TOK], vpad[:, 2 * b + mt, 2 * j + g, :],
                               probs[:, u % 2, j, mt, :], start=(g == 0 and mt == 0), stop=(g == 1 and mt == 1),
                               skip_group_check=True)
                else:
                    pe.wait_ge(paired, slots_before(p, u % 4 + 1))
                    for j in range(4):
                        last = mm(PS[head_rows(j), PV_BANK[b], TOK:2 * TOK], ones_par[:, g, :],
                                  pairs[:, u % 2, j, :], start=False, stop=(g == 1), skip_group_check=True)
                    last.then_inc(pv_done, 1)

            def logits(p):
                pe.wait_ge(xn_ready, NHALF + p + 1)
                for t in range(TILES):
                    last = mm(PS[:, GATE_BANK, t * E:(t + 1) * E], xn[:, p * HALF + t * 128:p * HALF + (t + 1) * 128],
                              gate_sb[:, :], start=True, stop=True)
                last.then_inc(logits_done, 1)

            def comb_rows(p):
                pe.wait_ge(comb_ready, p + 1)
                for t in range(TILES):
                    last = nc.tensor.transpose(PS[0:E, GATE_BANK, t * 128:(t + 1) * 128], comb[:, p, t, :], ident)
                last.then_inc(combT_done, 1)

            def up(n, k, s):
                w, m = wst[s // MT], s % MT
                p = k // E if isinstance(k, int) else 1
                if m == 0:
                    pe.wait_ge(wlo1_ready, k + 1)
                if not (isinstance(n, int) and n < 2):
                    pe.wait_ge(gelu_done, n - 1)
                if isinstance(n, int) and n % (MT * E) == 0:
                    pe.wait_ge(x2h_ready, p + 1)
                if isinstance(n, int) and n == 0:
                    pe.wait_ge(lo_ready, 6)
                o, ms = PS[:, U_BANK[s % 2], :], slice(m * 128, (m + 1) * 128)
                mm(o, w[0][:, ms], x2h[:, cols(p)], start=True, stop=False)
                mm(o, w[1][:, ms], x2h[:, cols(p)], start=False, stop=False)
                if isinstance(n, int) and n % (MT * E) == 0:
                    pe.wait_ge(x2l_ready, p + 1)
                mm(o, w[0][:, ms], x2l[:, cols(p)], start=False, stop=True).then_inc(up_done, 1)

            def down(n, k, s):
                w, m = wst[s // MT], s % MT
                if m == 0:
                    pe.wait_ge(wlo2_ready, k + 1)
                    if not (isinstance(k, int) and k < 2):
                        pe.wait_ge(part_ready, k - 1)
                pe.wait_ge(hl_ready, n + 1)
                o, ms = PS[:, Y_BANK[s // MT], :], slice(m * 128, (m + 1) * 128)
                mm(o, w[2][:, ms], hh[s % HR][:, :], start=(m == 0), stop=False)
                mm(o, w[3][:, ms], hh[s % HR][:, :], start=False, stop=False)
                mm(o, w[2][:, ms], hl[s % HR][:, :], start=False, stop=(m == MT - 1)).then_inc(down_done, 1)

            pe.wait_ge(cst_in, 64)
            for kt in range(2):
                pe.wait_ge(AT_in[2 * kt], 16)
                pe.wait_ge(AT_in[2 * kt + 1], 16)
                for b in range(2):
                    conv_apply(b, kt)
            for kt in range(2):
                conv_apply(2, kt)
            norm_mean(0)
            for kt in range(2):
                conv_apply(3, kt)
            norm_var(0)
            norm_spread(0)
            pe.wait_ge(attw_in, 16)
            for n in range(4):
                project(0, n)
            project_v(0)
            for t in range(TILES):
                for s in range(SLOTS[0]):
                    raw_scores(t, s)
            max_transpose(0)
            for s in range(SLOTS[0]):
                scores(0, s)
            for u in range(4):
                if u == 0:
                    norm_mean(1)
                if u == 1:
                    norm_var(1)
                if u == 2:
                    norm_spread(1)
                if u < 3:
                    for s in range(SLOTS[0]):
                        scores(u + 1, s)
                attend(u, 0)
                attend(u, 1)
            project(1, 0)
            project(1, 1)
            norm_mean(2)
            project(1, 2)
            norm_var(2)
            norm_spread(2)
            project(1, 3)
            project_v(1)

            for n in range(MT * FREE):
                for t, s in raw_slots(n):
                    raw_scores(t, s)
                if n == RAW0 + RAW_STEPS:
                    max_transpose(1)
                if scores_unit(n):
                    for s in range(3):
                        scores(scores_unit(n), s)
                up(n, n // MT, n % (2 * MT))
                if scores_unit(n):
                    scores(scores_unit(n), 3)
                for p in range(NHALF):
                    g = n - GATING[p]
                    if g == G_LOGITS:
                        logits(p)
                    if g == G_ROWS:
                        comb_rows(p)
                if n == NORM:
                    norm_mean(3)
                if n >= LAG:
                    down(n - LAG, (n - LAG) // MT, (n - LAG) % (2 * MT))
                if attend_unit(n):
                    attend(attend_unit(n), 0)
                    attend(attend_unit(n), 1)
                if n == NORM + 1:
                    norm_var(3)
                if n == NORM + 2:
                    norm_spread(3)
            with pe.Fori(FREE // 2, VISITS // 2) as i:
                for s in range(2 * MT):
                    up(2 * MT * i + s, 2 * i + s // MT, s)
                    back = (s - LAG) % (2 * MT)
                    down(2 * MT * i + s - LAG, 2 * i + (s - LAG) // MT, back)
            for n in range(MT * VISITS - LAG, MT * VISITS):
                down(n, n // MT, n % (2 * MT))


def kernel(**inputs):
    import concourse.bacc as bacc
    from concourse.bass_utils import run_bass_kernel_spmd

    a = {k: np.asarray(v) for k, v in inputs.items()}

    def by_parity(w):
        w = w.reshape(C, HEADS // 2, 2, 1, DK).transpose(0, 2, 1, 3, 4)
        return np.broadcast_to(w, (C, 2, HEADS // 2, 2, DK)).reshape(C, 256)

    consts = np.zeros((128, CONSTS), np.float32)
    consts[:, ID0:ID0 + 128] = np.eye(128)
    consts[:, AVG0:AVG0 + 128] = 1.0 / C
    consts[:, ONE0:ONE0 + DK] = 1.0
    consts[:, ONE0 + 32 + DK:ONE0 + 64] = 1.0
    consts[:, MASK0] = np.where(np.arange(128) % 32 < DK, 0.0, -1.0)
    consts[:, MASK0 + 1] = np.arange(128) % 32 < DK
    consts[:, MASK0 + 2] = np.arange(128) % 32 == DK
    consts[:, INDEX0:INDEX0 + E] = np.arange(E)

    arrays = {
        "x": a["x"].reshape(B, C, TOK).transpose(1, 0, 2).reshape(C, T),
        "x_kh": a["x"].reshape(B, C, H, KQ, K4).transpose(1, 0, 3, 2, 4).reshape(C, T),
        "convw": np.concatenate([a["L0_conv_wq"].T, np.zeros((C, 32 - C8), np.float32), a["L0_conv_wk"].T,
                                 a["L0_conv_wv"].T], axis=1),
        "convb": np.stack([np.pad(a["L0_conv_bq"], (0, 32)), np.pad(a["L0_conv_bk"], (32, 0))], axis=1),
        "bv": a["L0_conv_bv"],
        "gamma": a["L0_conv_gamma"],
        "attw": np.concatenate([by_parity(a["L1_attn_Wk"]), by_parity(a["L1_attn_Wq"]), a["L1_attn_Wv"]], axis=1),
        "gate": a["L1_ffn_gate_w"].T,
        "w12": np.concatenate([a["L1_ffn_w1"].transpose(0, 2, 1),
                               a["L1_ffn_w2"].reshape(E, C, MT, 128).transpose(0, 3, 2, 1).reshape(E, 128, HID)],
                              axis=2),
        "b1": a["L1_ffn_b1"].reshape(E, MT, 128).transpose(2, 0, 1).reshape(128, E * MT),
        "b2": a["L1_ffn_b2"].T,
        "consts": consts,
    }
    arrays = {k: np.ascontiguousarray(v) for k, v in arrays.items()}
    nc = bacc.Bacc("TRN2", target_bir_lowering=False, num_devices=1)
    args = [nc.dram_tensor(k, v.shape, mybir.dt.from_np(v.dtype), kind="ExternalInput").ap()
            for k, v in arrays.items()]
    out = nc.dram_tensor("out", (C, T), mybir.dt.float32, kind="ExternalOutput").ap()
    hybrid_program(nc, *args, out)
    r = run_bass_kernel_spmd(nc, [arrays], core_ids=[0])
    return r.results[0]["out"].reshape(C, B, H, W).transpose(1, 0, 2, 3)
```
